# Optimizing a Trainium2 kernel written in Bass

```python
import numpy as np
import jax
import jax.numpy as jnp

def _softmax(x, axis=-1):
    return jax.nn.softmax(x, axis=axis)

def _gelu(x):
    return jax.nn.gelu(x, approximate=True)

def _silu(x):
    return jax.nn.silu(x)

def _sigmoid(x):
    return jax.nn.sigmoid(x)

def _layernorm(x, axis=-1, eps=1e-05):
    m = jnp.mean(x, axis=axis, keepdims=True)
    v = jnp.var(x, axis=axis, keepdims=True)
    return (x - m) / jnp.sqrt(v + eps)

def _scatter_add(tgt, idx, src, axis=0):
    return tgt.at[idx].add(src)

def _segment_sum(src, seg, n):
    return jax.ops.segment_sum(src, seg, n)
kernel_name = 'mk_recurrent_d1_jaxref_r8_c19768'

def setup_inputs(seed: int=0):
    np.random.seed(seed)
    _w = jnp.asarray

    def _L0_attn_setup():
        import jax, jax.numpy as jnp
        import numpy as np
        B, S, E, H = (2, 256, 256, 16)
        NOPE, ROPE, VD = (128, 64, 128)
        QH = NOPE + ROPE
        LORA = 64
        ROPE_THETA = 10000.0
        EPS = 1e-06

        def _rope(xp, cos, sin):
            d2 = xp.shape[-1] // 2
            x1, x2 = (xp[..., :d2], xp[..., d2:])
            return jnp.concatenate([x1 * cos - x2 * sin, x2 * cos + x1 * sin], axis=-1)
        key = jax.random.key(seed)
        ks = jax.random.split(key, 5)
        sd = lambda n: 1.0 / np.sqrt(n)
        return {'x': jax.random.normal(ks[0], (B, S, E), jnp.float32), 'wq': jax.random.normal(ks[1], (E, H * QH), jnp.float32) * sd(E), 'wkv_a': jax.random.normal(ks[2], (E, LORA + ROPE), jnp.float32) * sd(E), 'wkv_b': jax.random.normal(ks[3], (LORA, H * (NOPE + VD)), jnp.float32) * sd(LORA), 'wo': jax.random.normal(ks[4], (H * VD, E), jnp.float32) * sd(H * VD), 'kv_norm_scale': jnp.ones((LORA,), jnp.float32)}
    _L0_attn_in = _L0_attn_setup()

    def _L0_ffn_setup():
        import jax, jax.numpy as jnp
        import numpy as np
        HIDDEN = 256
        INTER = 704
        B, S = (2, 256)

        def _ternary(key, shape):
            return jax.random.randint(key, shape, -1, 2).astype(jnp.float32)
        key = jax.random.key(seed)
        ks = jax.random.split(key, 7)
        x = jax.random.normal(ks[0], (B, S, HIDDEN), dtype=jnp.float32)
        gate_w = _ternary(ks[1], (INTER, HIDDEN))
        up_w = _ternary(ks[2], (INTER, HIDDEN))
        down_w = _ternary(ks[3], (HIDDEN, INTER))
        gate_s = jax.random.uniform(ks[4], (INTER,), minval=0.01, maxval=0.1, dtype=jnp.float32)
        up_s = jax.random.uniform(ks[5], (INTER,), minval=0.01, maxval=0.1, dtype=jnp.float32)
        down_s = jax.random.uniform(ks[6], (HIDDEN,), minval=0.01, maxval=0.1, dtype=jnp.float32)
        return {'x': x, 'gate_w': gate_w, 'up_w': up_w, 'down_w': down_w, 'gate_s': gate_s, 'up_s': up_s, 'down_s': down_s}
    _L0_ffn_in = _L0_ffn_setup()
    _d = {'L0_attn_x': _L0_attn_in['x'], 'L0_attn_wq': _L0_attn_in['wq'], 'L0_attn_wkv_a': _L0_attn_in['wkv_a'], 'L0_attn_wkv_b': _L0_attn_in['wkv_b'], 'L0_attn_wo': _L0_attn_in['wo'], 'L0_attn_kv_norm_scale': _L0_attn_in['kv_norm_scale'], 'L0_ffn_gate_w': _L0_ffn_in['gate_w'], 'L0_ffn_up_w': _L0_ffn_in['up_w'], 'L0_ffn_down_w': _L0_ffn_in['down_w'], 'L0_ffn_gate_s': _L0_ffn_in['gate_s'], 'L0_ffn_up_s': _L0_ffn_in['up_s'], 'L0_ffn_down_s': _L0_ffn_in['down_s']}
    _x0 = _d['L0_attn_x']
    _d['L0_attn_x'] = jax.random.normal(jax.random.fold_in(jax.random.key(seed), 1), (1, 2048, 256), dtype=_x0.dtype)
    del _x0
    return _d

def reference(L0_attn_x, L0_attn_wq, L0_attn_wkv_a, L0_attn_wkv_b, L0_attn_wo, L0_attn_kv_norm_scale, L0_ffn_gate_w, L0_ffn_up_w, L0_ffn_down_w, L0_ffn_gate_s, L0_ffn_up_s, L0_ffn_down_s):

    def _L0_attn_ref(x, wq, wkv_a, wkv_b, wo, kv_norm_scale):
        import jax, jax.numpy as jnp
        import numpy as np
        B, S, E, H = (2, 256, 256, 16)
        NOPE, ROPE, VD = (128, 64, 128)
        QH = NOPE + ROPE
        LORA = 64
        ROPE_THETA = 10000.0
        EPS = 1e-06

        def _rope(xp, cos, sin):
            d2 = xp.shape[-1] // 2
            x1, x2 = (xp[..., :d2], xp[..., d2:])
            return jnp.concatenate([x1 * cos - x2 * sin, x2 * cos + x1 * sin], axis=-1)
        b, s, _ = x.shape
        q = (x @ wq).reshape(b, s, H, QH).transpose(0, 2, 1, 3)
        q_nope, q_pe = (q[..., :NOPE], q[..., NOPE:])
        kva = x @ wkv_a
        ckv, k_pe = (kva[..., :LORA], kva[..., LORA:])
        ckv = ckv * jax.lax.rsqrt(jnp.mean(ckv * ckv, axis=-1, keepdims=True) + EPS)
        ckv = ckv * kv_norm_scale
        kv = (ckv @ wkv_b).reshape(b, s, H, NOPE + VD).transpose(0, 2, 1, 3)
        k_nope, v = (kv[..., :NOPE], kv[..., NOPE:])
        pos = jnp.arange(s, dtype=jnp.float32)
        inv = 1.0 / ROPE_THETA ** (jnp.arange(0, ROPE, 2, dtype=jnp.float32) / ROPE)
        ang = pos[:, None] * inv
        cos, sin = (jnp.cos(ang), jnp.sin(ang))
        q_pe = _rope(q_pe, cos, sin)
        k_pe = _rope(k_pe[:, None, :, :], cos, sin)
        qs = jnp.concatenate([q_nope, q_pe], axis=-1)
        ks_ = jnp.concatenate([k_nope, jnp.broadcast_to(k_pe, (b, H, s, ROPE))], axis=-1)
        scale = QH ** (-0.5)
        scores = jnp.einsum('bhqd,bhkd->bhqk', qs, ks_) * scale
        causal = jnp.tril(jnp.ones((s, s), dtype=bool))
        scores = jnp.where(causal, scores, jnp.finfo(scores.dtype).min)
        attn = jax.nn.softmax(scores, axis=-1)
        out = jnp.einsum('bhqk,bhkd->bhqd', attn, v)
        out = out.transpose(0, 2, 1, 3).reshape(b, s, H * VD)
        return out @ wo

    def _L0_ffn_ref(x, gate_w, up_w, down_w, gate_s, up_s, down_s):
        import jax, jax.numpy as jnp
        import numpy as np
        HIDDEN = 256
        INTER = 704
        B, S = (2, 256)

        def _ternary(key, shape):
            return jax.random.randint(key, shape, -1, 2).astype(jnp.float32)
        b, s, h = x.shape
        xf = x.reshape(b * s, h)
        g = jnp.einsum('th,ih->ti', xf, gate_w) * gate_s
        u = jnp.einsum('th,ih->ti', xf, up_w) * up_s
        hdn = jax.nn.silu(g) * u
        out = jnp.einsum('ti,hi->th', hdn, down_w) * down_s
        return out.reshape(b, s, -1)
    x = L0_attn_x
    xn = _layernorm(x, axis=-1)
    s = _L0_attn_ref(xn, L0_attn_wq, L0_attn_wkv_a, L0_attn_wkv_b, L0_attn_wo, L0_attn_kv_norm_scale)
    g = _silu(_L0_ffn_ref(xn, L0_ffn_gate_w, L0_ffn_up_w, L0_ffn_down_w, L0_ffn_gate_s, L0_ffn_up_s, L0_ffn_down_s))
    x = x + s * g
    return x

_drawn_inputs = setup_inputs


def setup_inputs(seed=0):
    import zlib

    import numpy as np

    out = dict(_drawn_inputs(seed))
    spreads = {'L0_attn_kv_norm_scale': (1.0, 0.6)}
    factors = {'L0_ffn_up_s': 2.809}
    for name, (base, spread) in spreads.items():
        noise = np.random.default_rng([zlib.crc32(name.encode()), seed]).standard_normal(out[name].shape)
        drawn = base * np.exp(spread * noise) if base else spread * noise
        out[name] = jnp.asarray(drawn.astype(out[name].dtype))
    for name, factor in factors.items():
        out[name] = (out[name] * factor).astype(out[name].dtype)
    return out
```

```python
from contextlib import ExitStack

import concourse.bass as bass
import concourse.mybir as mybir

F32 = mybir.dt.float32
F32R = mybir.dt.float32r
F16 = mybir.dt.float16
BF16 = mybir.dt.bfloat16
ALU = mybir.AluOpType
ACT = mybir.ActivationFunctionType
AX = mybir.AxisListType

P = 128
S, E = 2048, 256
H, NOPE, ROPE, VD, LORA = 16, 128, 64, 128, 64
INTER = 704
EPS_LN, EPS_RMS = 1e-5, 1e-6
SCALE = float((NOPE + ROPE) ** -0.5)
MASKED = -3.0e38
NT = S // P
KE = E // P
BANK = 512
BLK = BANK // P
NG = NT // BLK
PAIRS = H // 2
QW = 2 * (NOPE + ROPE)
KVW = 2 * (NOPE + VD)
IT = -(-INTER // P)
SBANKS = 5
NP_RING, PT_RING, TILE_RING = 4, 5, 4
VW = 2 * LORA + 1

TILE_ORDER = [t for k in range(NT // 2) for t in (NT - 1 - k, k)]
CHUNKS = []
for pos, t in enumerate(TILE_ORDER):
    keys = (t + 1) * P
    for k0 in range(0, keys, BANK):
        CHUNKS.append((t, pos, k0, min(BANK, keys - k0), k0 == 0, k0 + BANK >= keys))
NCH = len(CHUNKS)
STEPS = 2 * NCH


WEIGH = {0: (-3,), 1: (-3,), 2: (-3,), 3: (), 4: (-4, -3)}


def weigh_at(step):
    return [step + d for d in WEIGH[step % SBANKS] if step + d >= 0]


WEIGH_END = range(STEPS - 3, STEPS)


def chunk(g):
    g %= STEPS
    t, pos, k0, w, first, last = CHUNKS[g % NCH]
    head = g // NCH
    return head, t, head * NT + pos, k0, w, first, last


class Slots:

    def __init__(self):
        self.kinds, self.counts, self.at = [], [], {}
        self.count = {"ready": 0, "hi": 0, "act": 0, "dve": 0}

    def add(self, name, kind):
        self.count["ready"] += 1
        if kind == "split":
            self.count["hi"] += 1
        self.count["act" if kind == "act" else "dve"] += 1
        self.kinds.append(kind)
        self.counts.append(dict(self.count))
        self.at[name] = len(self.kinds) - 1


class Phase:

    def __init__(self, slots, pool, base, pool_base, pair=None):
        self.slots, self.pool, self.base, self.pool_base, self.pair = slots, pool, base, pool_base, pair

    def of_pair(self, pair):
        base = {k: self.base[k] + pair * self.slots.count[k] for k in self.base}
        return Phase(self.slots, self.pool, base, self.pool_base + pair * len(self.pool.names), pair)

    def after(self, kind, name):
        return self.base[kind] + self.slots.counts[self.slots.at[name]][kind]

    def pool_after(self, name):
        return self.pool_base + self.pool.after[name]

    def end(self, times=1):
        return {k: self.base[k] + times * self.slots.count[k] for k in self.base}


SPLIT, BY_ACT, BY_DVE = "split", "act", "dve"

OUT_JOBS = {1: ("outT3", SPLIT), 3: ("outP3a", BY_DVE), 5: ("outP3b", BY_DVE), 8: ("wvo", SPLIT),
            56: ("outT0", SPLIT), 58: ("outP0a", BY_DVE), 60: ("outP0b", BY_DVE),
            66: ("outT1", SPLIT), 68: ("outP1a", BY_DVE), 70: ("outP1b", BY_DVE),
            75: ("outT2", SPLIT), 77: ("outP2a", BY_DVE), 79: ("outP2b", BY_DVE)}
PREP_JOBS = {11: ("wqT", BY_ACT), 14: ("wkvT", BY_ACT), 16: ("pe0", BY_ACT), 18: ("wabs", SPLIT), 20: ("pe1", BY_ACT),
             22: ("lat0", BY_ACT), 24: ("pe2", BY_ACT), 26: ("peT0", BY_ACT), 28: ("lat1", BY_ACT),
             30: ("pe3", BY_ACT), 32: ("peT1", BY_ACT), 34: ("lat2", BY_ACT), 37: ("peT2", BY_ACT),
             39: ("lat3", BY_ACT), 42: ("peT3", BY_ACT)}
OUT_LAST = [OUT_JOBS[s] for s in (1, 3, 5)]
PREP_FIRST = [("wqT", BY_ACT), ("pe0", BY_ACT), ("wkvT", BY_ACT), ("pe1", BY_ACT), ("wabs", SPLIT),
              ("pe2", BY_ACT), ("peT0", BY_ACT), ("pe3", BY_ACT), ("lat0", BY_ACT), ("peT1", BY_ACT),
              ("lat1", BY_ACT), ("peT2", BY_ACT), ("lat2", BY_ACT), ("peT3", BY_ACT), ("lat3", BY_ACT)]


def job_at(step, prep):
    return OUT_JOBS.get(step) or (PREP_JOBS.get(step) if prep else None)


def pair_slots(prep):
    slots = Slots()
    for s in range(STEPS):
        slots.add(("T", s), SPLIT)
        if job_at(s, prep):
            slots.add(*job_at(s, prep))
    assert len(slots.kinds) % 2 == 0 or not prep
    return slots


SETUP = Slots()
for n in range(NG):
    for k in range(KE):
        SETUP.add(("xT", n, k), SPLIT)
for n in range(NG):
    SETUP.add(("kv", n), BY_ACT)
for n in range(NG):
    for side in "BA":
        SETUP.add(("K", n, side), SPLIT)
for name, kind in PREP_FIRST:
    SETUP.add(name, kind)
if len(SETUP.kinds) % 2:
    SETUP.add("pad", BY_ACT)
LOOP, LAST = pair_slots(True), pair_slots(False)
TAIL = Slots()
for name, kind in OUT_LAST:
    TAIL.add(name, kind)
FFN_UP = [(w, k, half) for w in range(2) for k in range(KE) for half in range(2)]
FFN_DOWN = [(2, i) for i in range(IT // 2)]
for name in FFN_UP + FFN_DOWN:
    TAIL.add(name, SPLIT)

POOL_SETUP = ["half", "ones", "ident0", "ident"] + [f"rstd{n}" for n in range(NG)] + ["identb", "mask0", "mask"] + [
    x for n in range(NG) for x in [f"rms{n}"] + [f"kr{n}.{i}" for i in range(6)]]
POOL_W = ["wpe_hi", "wpe_lo", "wkvs"]
POOL_QB = ["qb_lat_hi", "qb_lat_lo", "qb_pe_hi", "qb_pe_lo"]
POOL_ROPE = [f"rope{n}.{i}" for n in range(NG) for i in range(5)]
POOL_QA = ["qa_lat_hi", "qa_lat_lo", "qa_pe_hi", "qa_pe_lo"]


class Steps:

    def __init__(self, names):
        self.names = names
        self.after = {n: i + 1 for i, n in enumerate(names)}


POOL_PRO = Steps(POOL_SETUP + POOL_W + POOL_ROPE + POOL_QA)
POOL_LOOP = Steps(POOL_QB + POOL_W + POOL_ROPE + POOL_QA)
POOL_LAST = Steps(POOL_QB)


def mla_gated_ffn_kernel(nc, x, wq, wkv_a, wkv_b, wo, kv_scale, gate_w, up_w, down_w, gate_s, up_s,
                         down_s, cos_in, sin_in, out):
    with ExitStack() as ctx:
        def sem(name):
            return ctx.enter_context(nc.semaphore(name))

        def sb(name, shape, dt=F32, where=ctx):
            return where.enter_context(nc.sbuf_tensor(name, shape, dt))

        xT_hi = sb("xT_hi", [P, KE, S], F32R)
        xT_lo = sb("xT_lo", [P, KE, S], F32R)
        acc = sb("acc", [P, NT, E])
        ident = sb("ident", [P, P])

        attn = ExitStack()

        def ab(name, shape, dt=F32):
            return sb(name, shape, dt, attn)

        K_hi = [ab(f"K{h}_hi", [P, S], F32R) for h in "AB"]
        K_lo = [ab(f"K{h}_lo", [P, S], F32R) for h in "AB"]
        v = ab("v", [P, NT, VW + 1], F16)
        wq_sb = ab("wq_sb", [P, KE, QW])
        wpe_hi = ab("wpe_hi", [P, KE, 2, ROPE], F32R)
        wpe_lo = ab("wpe_lo", [P, KE, 2, ROPE], F32R)
        wqT = ab("wqT", [P, 2, KE, P])
        wkv_sb = ab("wkv_sb", [LORA, KVW])
        wkvs = ab("wkvs", [P, KVW])
        ones = ab("ones", [P, 1])
        spare = ab("spare", [P, 2])
        wkT = ab("wkT", [P, 2, LORA])
        wvT = ab("wvT", [P, 2, P])
        wo_sb = ab("wo_sb", [P, 2, E])
        wabs_hi = ab("wabs_hi", [P, KE, P], F32R)
        wabs_lo = ab("wabs_lo", [P, KE, P], F32R)
        wvo_hi = ab("wvo_hi", [P, E], F32R)
        wvo_lo = ab("wvo_lo", [P, E], F32R)
        cos_sb = ab("cos_sb", [P, NT, ROPE // 2])
        sin_sb = ab("sin_sb", [P, NT, ROPE // 2])
        scale_sb = ab("scale_sb", [LORA, 1])
        mask = ab("mask", [P, P], BF16)
        identb = ab("identb", [P, P], BF16)
        part_max = ab("part_max", [P, TILE_RING, BLK])
        neg_max = ab("neg_max", [P, TILE_RING])
        rinv = ab("rinv", [P, 2, 2])

        late = ExitStack()

        def lb(name, shape, dt=F32):
            return sb(name, shape, dt, late)

        Q_hi = [lb(f"Q{h}_hi", [P, S], F32R) for h in "AB"]
        Q_lo = [lb(f"Q{h}_lo", [P, S], F32R) for h in "AB"]
        lat = lb("lat", [P, S])
        pe = lb("pe", [P, S])
        prob = lb("prob", [P, NP_RING, BANK])
        pT_hi = lb("pT_hi", [P, PT_RING, BANK], F16)
        pT_lo = lb("pT_lo", [P, PT_RING, BANK], F16)
        o_raw = lb("o_raw", [P, 2, 2, VW])
        o_sum = lb("o_sum", [P, 2, 2, LORA])
        o_pair = lb("o_pair", [P, NT, P])
        oT_hi = lb("oT_hi", [P, 2, BANK], F32R)
        oT_lo = lb("oT_lo", [P, 2, BANK], F32R)
        qtok = lb("qtok", [P, 2, BLK, P])
        qrot = lb("qrot", [P, 2, BLK, P])
        rope_c = lb("rope_c", [P, BLK, P])
        rope_s = lb("rope_s", [P, BLK, P])
        late.close()

        setup = ExitStack()

        def ub(name, shape, dt=F32):
            return sb(name, shape, dt, setup)

        wkva_sb = ub("wkva_sb", [P, KE, P])
        wkva_hi = ub("wkva_hi", [P, KE, P], F32R)
        wkva_lo = ub("wkva_lo", [P, KE, P], F32R)
        kraw = ub("kraw", [P, NT, P])
        kcat = ub("kcat", [P, NT, 3 * LORA])
        kn = ub("kn", [P, NT, LORA])
        sq = ub("sq", [P, BLK, LORA])
        krope_c = ub("krope_c", [P, NT, ROPE])
        krope_s = ub("krope_s", [P, NT, ROPE])
        krot = ub("krot", [P, NT, ROPE])
        stat = ub("stat", [P, NT, 6])
        mv = ub("mv", [P, NT, 2])
        var_eps = ub("var_eps", [P, NT])
        minus_half = ub("minus_half", [P, BLK])
        rstd = ub("rstd", [P, NT])
        ss = ub("ss", [P, NT])
        ms_eps = ub("ms_eps", [P, NT])
        rms = ub("rms", [P, NT])
        setup.close()
        attn.close()

        ffn = ExitStack()

        def fb(name, shape, dt=F32):
            return sb(name, shape, dt, ffn)

        up_raw = fb("up_raw", [P, 2, IT, E])
        down_raw = fb("down_raw", [P, KE, IT * P])
        upT_hi = fb("upT_hi", [P, 2, KE, IT * P], F32R)
        upT_lo = fb("upT_lo", [P, 2, KE, IT * P], F32R)
        downT_hi = fb("downT_hi", [P, IT, E], F32R)
        downT_lo = fb("downT_lo", [P, IT, E], F32R)
        silu_g = fb("silu_g", [P, 2, BANK])
        hid = fb("hid", [P, 2, BANK])
        hid_hi = fb("hid_hi", [P, 2, IT, BANK], F32R)
        hid_lo = fb("hid_lo", [P, 2, IT, BANK], F32R)
        up_scale = fb("up_scale", [P, 2, IT])
        down_scale = fb("down_scale", [P, KE])
        gate = fb("gate", [P, 2, 2, E])
        x_in = fb("x_in", [P, NT, E])
        y = fb("y", [P, 2, 2, E])
        ffn.close()

        s_ps = ctx.enter_context(nc.psum_tensor("s_ps", [P, SBANKS, BANK], F32))
        slot_ps = ctx.enter_context(nc.psum_tensor("slot_ps", [P, 2, BANK], F32))
        o_ps = ctx.enter_context(nc.psum_tensor("o_ps", [P, BANK], F32))

        x_loaded = [sem(f"x_loaded{n}") for n in range(NG)]
        consts_loaded = sem("consts_loaded")
        wq_loaded, wkv_loaded, wo_loaded = sem("wq_loaded"), sem("wkv_loaded"), sem("wo_loaded")
        slot_ready, hi_done = sem("slot_ready"), sem("hi_done")
        act_freed, dve_freed = sem("act_freed"), sem("dve_freed")
        pool_done = sem("pool_done")
        dve_setup = sem("dve_setup")
        xn_done = sem("xn_done")
        kcat_done = sem("kcat_done")
        wkva_done = sem("wkva_done")
        scores_ready = sem("scores_ready")
        part_done = sem("part_done")
        max_ready = sem("max_ready")
        exp_done = sem("exp_done")
        pv_done = sem("pv_done")

        o_copied = sem("o_copied")
        summed = sem("summed")
        norm_done = sem("norm_done")
        ffn_loaded = sem("ffn_loaded")
        ffn_zero, ffn_scaled = sem("ffn_zero"), sem("ffn_scaled")
        gu_ready, silu_done, hid_done = sem("gu_ready"), sem("silu_done"), sem("hid_done")
        hid_hi_done, hid_lo_done = sem("hid_hi_done"), sem("hid_lo_done")
        down_ready, gate_done = sem("down_ready"), sem("gate_done")
        gated, y_done = sem("gated"), sem("y_done")
        stored = [sem("stored0"), sem("stored1")]
        x_again = sem("x_again")

        setup_ph = Phase(SETUP, POOL_PRO, {"ready": 0, "hi": 0, "act": 0, "dve": 0}, 0)
        loop_ph = Phase(LOOP, POOL_LOOP, setup_ph.end(), len(POOL_PRO.names))
        last_ph = Phase(LAST, POOL_LAST, loop_ph.end(PAIRS - 1),
                        loop_ph.pool_base + (PAIRS - 1) * len(POOL_LOOP.names), PAIRS - 1)
        tail_ph = Phase(TAIL, None, last_ph.end(), 0)
        PARTS = sum(not (c[4] and c[5]) for c in CHUNKS) * 2
        part_of = {}
        for g in range(STEPS):
            first, last = chunk(g)[5:]
            part_of[g] = len([i for i in part_of.values() if i]) + 1 if not (first and last) else 0

        block = ctx.enter_context(nc.Block())

        @block.sync
        def _(sp):
            xv = x[0].rearrange("(t p) d -> p t d", p=P)
            for n in range(NG):
                sp.dma_start(acc[:, BLK * n:BLK * n + BLK, :], xv[:, BLK * n:BLK * n + BLK, :]).then_inc(x_loaded[n], 16)
            sp.dma_start(wkva_sb[:], wkv_a.rearrange("(k e) c -> e k c", k=KE)).then_inc(consts_loaded, 16)
            sp.dma_start(cos_sb[:], cos_in.rearrange("(t p) d -> p t d", p=P)).then_inc(consts_loaded, 16)
            sp.dma_start(sin_sb[:], sin_in.rearrange("(t p) d -> p t d", p=P)).then_inc(consts_loaded, 16)
            sp.dma_start(scale_sb[:], kv_scale.rearrange("(l o) -> l o", o=1)).then_inc(consts_loaded, 16)

            def load(pair):
                wqv = wq.rearrange("(k e) n -> e k n", k=KE)
                sp.dma_start(wq_sb[:], wqv[:, :, bass.ds(pair * QW, QW)]).then_inc(wq_loaded, 16)
                sp.dma_start(wkv_sb[:], wkv_b[:, bass.ds(pair * KVW, KVW)]).then_inc(wkv_loaded, 16)

            def load_wo(pair):
                wov = wo.rearrange("(h d) n -> d h n", d=VD)
                sp.dma_start(wo_sb[:], wov[:, bass.ds(pair * 2, 2), :]).then_inc(wo_loaded, 16)

            load(0)
            load_wo(0)
            with sp.Fori(0, PAIRS - 1) as p:
                ph = loop_ph.of_pair(p)
                sp.wait_ge(slot_ready, ph.base["ready"])
                sp.wait_ge(pool_done, ph.pool_base)
                load(p + 1)
                sp.wait_ge(slot_ready, ph.after("ready", "wvo"))
                load_wo(p + 1)

            sp.wait_ge(slot_ready, tail_ph.after("ready", "outP3b"))
            sp.wait_ge(ffn_zero, 1)
            sp.wait_ge(pool_done, last_ph.pool_base + len(POOL_LAST.names))
            sp.wait_ge(dve_freed, tail_ph.after("dve", "outP3b"))
            whole = INTER // P
            rest = INTER - whole * P
            for w, src in enumerate((gate_w, up_w)):
                sp.dma_start(up_raw[:, w, 0:whole, :], src[0:whole * P, :].rearrange("(t p) e -> p t e", p=P)).then_inc(ffn_loaded, 16)
                sp.dma_start(up_raw[0:rest, w, whole, :], src[whole * P:INTER, :]).then_inc(ffn_loaded, 16)
            for w, src in enumerate((gate_s, up_s)):
                with nc.allow_non_contiguous_dma(reason="scales, one value to a partition"):
                    sp.dma_start(up_scale[:, w, 0:whole], src[0:whole * P].rearrange("(t p) -> p t", p=P)).then_inc(ffn_loaded, 16)
                    sp.dma_start(up_scale[0:rest, w, whole:whole + 1], src[whole * P:INTER].rearrange("(p o) -> p o", o=1)).then_inc(ffn_loaded, 16)
            sp.dma_start(down_raw[:, :, 0:INTER], down_w.rearrange("(k p) i -> p k i", p=P)).then_inc(ffn_loaded, 16)
            with nc.allow_non_contiguous_dma(reason="scales, one value to a partition"):
                sp.dma_start(down_scale[:], down_s.rearrange("(k p) -> p k", p=P)).then_inc(ffn_loaded, 16)
            sp.dma_start(x_in[:], xv).then_inc(x_again, 16)
            yv = out[0].rearrange("(t p) d -> p t d", p=P)
            for u in range(2 * NG):
                sp.wait_ge(y_done, u + 1)
                sp.dma_start(yv[:, 2 * u:2 * u + 2, :], y[:, u % 2]).then_inc(stored[u % 2], 16)
            for done in stored:
                sp.wait_ge(done, 16 * NG)

        @block.tensor
        def _(pe_eng):
            def slot(ph, name):
                i = ph.slots.at[name]
                if i >= 2:
                    freed = "act" if ph.slots.kinds[i - 2] == BY_ACT else "dve"
                    pe_eng.wait_ge(act_freed if freed == "act" else dve_freed,
                                   ph.base[freed] + ph.slots.counts[i - 2][freed])
                elif ph is not setup_ph and i == 0:
                    pe_eng.wait_ge(act_freed, ph.base["act"])
                    pe_eng.wait_ge(dve_freed, ph.base["dve"])
                return slot_ps[:, i % 2, :]

            def exact(out_ap, parts):
                n = 3 * len(parts)
                i = 0
                for a_hi, a_lo, b_hi, b_lo in parts:
                    for a, b in ((a_hi, b_hi), (a_hi, b_lo), (a_lo, b_hi)):
                        last = nc.tensor.matmul(out_ap, a, b, start=(i == 0), stop=(i == n - 1))
                        i += 1
                return last

            def x_tile(t):
                return [(xT_hi[:, k, t * P:(t + 1) * P], xT_lo[:, k, t * P:(t + 1) * P]) for k in range(KE)]

            def prep_job(ph, name, pair_after):
                ps = slot(ph, name)
                if name == "wqT":
                    pe_eng.wait_ge(wq_loaded, 16 * pair_after)
                    for h in range(2):
                        for k in range(KE):
                            c = h * (NOPE + ROPE)
                            last = nc.tensor.transpose(ps[:, (h * KE + k) * P:(h * KE + k + 1) * P], wq_sb[:, k, c:c + NOPE], ident[:])
                elif name == "wkvT":
                    pe_eng.wait_ge(pool_done, ph.pool_after("wkvs"))
                    for i in range(4):
                        last = nc.tensor.transpose(ps[:, i * P:(i + 1) * P], wkvs[:, i * P:(i + 1) * P], ident[:])
                elif name == "wabs":
                    pe_eng.wait_ge(act_freed, ph.after("act", "wkvT"))
                    for k in range(KE):
                        for h in (1, 0):
                            c = k * P + (1 - h) * LORA
                            last = nc.tensor.matmul(ps[:, c:c + LORA], wqT[:, h, k, :], wkT[:, h, :], start=True, stop=True)
                elif name.startswith("lat"):
                    n = int(name[3:])
                    pe_eng.wait_ge(dve_freed, ph.after("dve", "wabs"))
                    c = slice(n * BANK, (n + 1) * BANK)
                    last = exact(ps, [(wabs_hi[:, k, :], wabs_lo[:, k, :], xT_hi[:, k, c], xT_lo[:, k, c]) for k in range(KE)])
                elif name.startswith("peT"):
                    n = int(name[3:])
                    pe_eng.wait_ge(pool_done, ph.pool_after(f"rope{n}.4"))
                    for j in range(BLK):
                        last = nc.tensor.transpose(ps[:, j * P:(j + 1) * P], qrot[:, n % 2, j, :], ident[:])
                else:
                    n = int(name[2:])
                    pe_eng.wait_ge(pool_done, ph.pool_after("wpe_lo"))
                    for j in range(BLK):
                        w = [(wpe_hi[:, k, :, :].rearrange("p h c -> p (h c)"), wpe_lo[:, k, :, :].rearrange("p h c -> p (h c)")) for k in range(KE)]
                        last = exact(ps[:, j * P:(j + 1) * P], [(*a, *b) for a, b in zip(x_tile(BLK * n + j), w)])
                last.then_inc(slot_ready, 1)

            def out_job(ph, name, pair):
                if name == "wvo":
                    ps = slot(ph, name)
                    pe_eng.wait_ge(wo_loaded, 16 * (pair + 1))
                    for h in range(2):
                        last = nc.tensor.matmul(ps[:, 0:E], wvT[:, h, :], wo_sb[:, h, :], start=(h == 0), stop=(h == 1))
                    last.then_inc(slot_ready, 1)
                    return
                q = int(name[4])
                if name.startswith("outT"):
                    ps = slot(ph, name)
                    done = 1 + NT * pair if q == NG - 1 else 1 + NT * pair + NT // 2 + 2 * q + 2
                    pe_eng.wait_ge(norm_done, done)
                    for j in range(BLK):
                        last = nc.tensor.transpose(ps[:, j * P:(j + 1) * P], o_pair[:, TILE_ORDER[4 * q + j], :], ident[:])
                else:
                    half = "ab".index(name[5])
                    ps = slot(ph, name)
                    pe_eng.wait_ge(dve_freed, ph.after("dve", f"outT{q}"))
                    for i, j in enumerate((2 * half + 1, 2 * half)):
                        c = slice(j * P, (j + 1) * P)
                        last = exact(ps[:, i * E:(i + 1) * E], [(oT_hi[:, q % 2, c], oT_lo[:, q % 2, c], wvo_hi[:], wvo_lo[:])])
                last.then_inc(slot_ready, 1)

            def scores(g, queries_ready):
                head, t, _, k0, w, first, last_chunk = chunk(g)
                if g % NCH == 0:
                    pe_eng.wait_ge(pool_done, queries_ready)
                out_ap = s_ps[:, g % SBANKS, 0:w]
                q = slice(t * P, (t + 1) * P)
                for i, (a, b) in enumerate(((Q_hi, K_hi), (Q_hi, K_lo), (Q_lo, K_hi))):
                    mm = nc.tensor.matmul(out_ap, a[head][:, q], b[head][:, k0:k0 + w],
                                          start=(i == 0), stop=(i == 2 and not last_chunk))
                if last_chunk:
                    mm = nc.tensor.matmul(out_ap[:, w - P:w], identb[:], mask[:], start=False, stop=True)
                mm.then_inc(scores_ready, 1)

            def turn(ph, g):
                ps = slot(ph, ("T", g))
                pe_eng.wait_ge(exp_done, ph.pair * STEPS + g + 1)
                for b in range(chunk(g)[4] // P):
                    last = nc.tensor.transpose(ps[:, b * P:(b + 1) * P], prob[:, g % NP_RING, b * P:(b + 1) * P], ident[:])
                last.then_inc(slot_ready, 1)

            def weigh(ph, g):
                _, _, tile_no, k0, w, first, last_chunk = chunk(g)
                pe_eng.wait_ge(dve_freed, ph.after("dve", ("T", g)))
                if g % SBANKS == 0:
                    pe_eng.wait_ge(o_copied, 1 + ph.pair * NT + g // SBANKS)
                c0 = tile_no % 2 * VW
                n = w // P
                for b in range(n):
                    kb = k0 // P + b
                    c = slice(b * P, (b + 1) * P)
                    hi, lo = pT_hi[:, g % PT_RING, c], pT_lo[:, g % PT_RING, c]
                    nc.tensor.matmul(o_ps[:, c0:c0 + VW], hi, v[:, kb, 0:VW], start=(first and b == 0), stop=False)
                    last = nc.tensor.matmul(o_ps[:, c0:c0 + LORA + 1], lo, v[:, kb, 0:LORA + 1], start=False, stop=(last_chunk and b == n - 1))
                last.then_inc(pv_done, 1)

            def pair_program(ph, prep):
                for s in range(STEPS):
                    turn(ph, s)
                    if s + SBANKS < STEPS:
                        scores(s + SBANKS, ph.pool_after("qb_pe_lo"))
                    elif prep:
                        scores(s + SBANKS, ph.pool_after("qa_pe_lo"))
                    if s in OUT_JOBS:
                        out_job(ph, OUT_JOBS[s][0], ph.pair)
                    elif prep and s in PREP_JOBS:
                        prep_job(ph, PREP_JOBS[s][0], ph.pair + 2)
                    for g in weigh_at(s):
                        weigh(ph, g)
                for g in WEIGH_END:
                    weigh(ph, g)

            ph = setup_ph
            pe_eng.wait_ge(pool_done, ph.pool_after("ident"))
            for n in range(NG):
                pe_eng.wait_ge(xn_done, BLK * (n + 1))
                for k in range(KE):
                    ps = slot(ph, ("xT", n, k))
                    for j in range(BLK):
                        last = nc.tensor.transpose(ps[:, j * P:(j + 1) * P], acc[:, BLK * n + j, k * P:(k + 1) * P], ident[:])
                    last.then_inc(slot_ready, 1)
            pe_eng.wait_ge(wkva_done, 2)
            for n in range(NG):
                ps = slot(ph, ("kv", n))
                pe_eng.wait_ge(dve_freed, ph.after("dve", ("xT", n, KE - 1)))
                for j in range(BLK):
                    last = exact(ps[:, j * P:(j + 1) * P], [(*a, wkva_hi[:, k, :], wkva_lo[:, k, :]) for k, a in enumerate(x_tile(BLK * n + j))])
                last.then_inc(slot_ready, 1)
            for n in range(NG):
                for side in "BA":
                    ps = slot(ph, ("K", n, side))
                    if side == "B":
                        pe_eng.wait_ge(kcat_done, n + 1)
                        pe_eng.wait_ge(pool_done, ph.pool_after(f"kr{n}.5"))
                    c = 0 if side == "B" else LORA
                    for j in range(BLK):
                        last = nc.tensor.transpose(ps[:, j * P:(j + 1) * P], kcat[:, BLK * n + j, c:c + P], ident[:])
                    last.then_inc(slot_ready, 1)
            for name, _ in PREP_FIRST:
                prep_job(ph, name, 1)
            if "pad" in SETUP.at:
                ps = slot(ph, "pad")
                nc.tensor.transpose(ps[:, 0:P], ident[:], ident[:]).then_inc(slot_ready, 1)
            for g in range(SBANKS):
                scores(g, ph.pool_after("qa_pe_lo"))
            with pe_eng.Fori(0, PAIRS - 1) as p:
                pair_program(loop_ph.of_pair(p), True)
            pair_program(last_ph, False)
            for name, _ in OUT_LAST:
                out_job(tail_ph, name, PAIRS)

            ph = tail_ph
            pe_eng.wait_ge(ffn_scaled, 4)
            for w, k, half in FFN_UP:
                ps = slot(ph, (w, k, half))
                for j in range(IT // 2):
                    last = nc.tensor.transpose(ps[:, j * P:(j + 1) * P], up_raw[:, w, half * (IT // 2) + j, k * P:(k + 1) * P], ident[:])
                last.then_inc(slot_ready, 1)
            for _, i in FFN_DOWN:
                ps = slot(ph, (2, i))
                for j in range(2):
                    for k in range(KE):
                        c = (2 * i + j) * P
                        last = nc.tensor.transpose(ps[:, j * E + k * P:j * E + (k + 1) * P], down_raw[:, k, c:c + P], ident[:])
                last.then_inc(slot_ready, 1)

            def gate_up(n):
                for it in range(IT):
                    j = n * IT + it
                    if j >= 2:
                        pe_eng.wait_ge(hid_done, j - 1)
                    for w in range(2):
                        if j == 0:
                            pe_eng.wait_ge(dve_freed, ph.after("dve", FFN_DOWN[-1]))
                        c = slice(n * BANK, (n + 1) * BANK)
                        i = slice(it * P, (it + 1) * P)
                        last = exact(s_ps[:, 2 * (j % 2) + w, :], [
                            (upT_hi[:, w, k, i], upT_lo[:, w, k, i], xT_hi[:, k, c], xT_lo[:, k, c]) for k in range(KE)])
                    last.then_inc(gu_ready, 1)

            def down(n):
                pe_eng.wait_ge(hid_lo_done, IT * (n + 1))
                for tp in range(2):
                    u = 2 * n + tp
                    if u >= 2:
                        pe_eng.wait_ge(gate_done, u - 1)
                    for j in range(2):
                        c = slice((2 * tp + j) * P, (2 * tp + j + 1) * P)
                        bank = s_ps[:, SBANKS - 1, :] if u % 2 else o_ps[:, :]
                        last = exact(bank[:, j * E:(j + 1) * E], [
                            (hid_hi[:, n % 2, it, c], hid_lo[:, n % 2, it, c], downT_hi[:, it, :], downT_lo[:, it, :]) for it in range(IT)])
                    last.then_inc(down_ready, 1)

            gate_up(0)
            for n in range(1, NG):
                gate_up(n)
                down(n - 1)
            down(NG - 1)

        @block.scalar
        def _(act):
            def copy(dst, src):
                return nc.scalar.activation(dst, src, ACT.Copy)

            def slot_of(ph, name):
                act.wait_ge(slot_ready, ph.after("ready", name))
                return slot_ps[:, ph.slots.at[name] % 2, :]

            def prep_job(ph, name):
                ps = slot_of(ph, name)
                if name == "wqT":
                    copy(wqT[:].rearrange("p h k e -> p (h k e)"), ps).then_inc(act_freed, 1)
                elif name == "wkvT":
                    blocks = ps.rearrange("p (h v c) -> p h v c", h=2, v=2)
                    copy(wkT[:], blocks[:, :, 0, 0:LORA])
                    copy(wvT[:, 0, 0:LORA], blocks[:, 0, 1, 0:LORA])
                    copy(wvT[:, 1, LORA:P], blocks[:, 1, 1, 0:LORA]).then_inc(act_freed, 1)
                elif name == "wabs":
                    copy(wabs_hi[:].rearrange("p k c -> p (k c)"), ps[:, 0:KE * P]).then_inc(hi_done, 1)
                elif name.startswith("lat"):
                    n = int(name[3:])
                    if ph is not setup_ph:
                        act.wait_ge(pool_done, ph.pool_after("qb_pe_lo"))
                    copy(lat[:, n * BANK:(n + 1) * BANK], ps).then_inc(act_freed, 1)
                elif name.startswith("peT"):
                    n = int(name[3:])
                    if ph is not setup_ph:
                        act.wait_ge(pool_done, ph.pool_after("qb_pe_lo"))
                    copy(pe[:, n * BANK:(n + 1) * BANK], ps).then_inc(act_freed, 1)
                elif name == "pad":
                    copy(spare[:, 0:1], ps[:, 0:1]).then_inc(act_freed, 1)
                else:
                    n = int(name[2:])
                    if n >= 2:
                        act.wait_ge(pool_done, ph.pool_after(f"rope{n - 2}.4"))
                    copy(qtok[:, n % 2].rearrange("p t c -> p (t c)"), ps).then_inc(act_freed, 1)

            def out_job(ph, name):
                if name == "wvo":
                    copy(wvo_hi[:], slot_of(ph, name)[:, 0:E]).then_inc(hi_done, 1)
                elif name.startswith("outT"):
                    copy(oT_hi[:, int(name[4]) % 2, :], slot_of(ph, name)).then_inc(hi_done, 1)

            def exponentials(pair, g):
                _, _, tile_no, _, w, first, _ = chunk(g)
                if first:
                    act.wait_ge(max_ready, (pair + g // STEPS) * 2 * NT + tile_no + 1)
                nc.scalar.activation(prob[:, g % NP_RING, 0:w], s_ps[:, g % SBANKS, 0:w], ACT.Exp,
                                     bias=neg_max[:, tile_no % TILE_RING:tile_no % TILE_RING + 1]).then_inc(exp_done, 1)

            def copy_outputs(ph, r):
                act.wait_ge(pv_done, ph.pair * STEPS + SBANKS * (r + 1))
                copy(o_raw[:, r % 2].rearrange("p t c -> p (t c)"), o_ps[:, 0:2 * VW]).then_inc(o_copied, 1)

            def turned_hi(ph, g):
                w = chunk(g)[4]
                copy(pT_hi[:, g % PT_RING, 0:w], slot_of(ph, ("T", g))[:, 0:w]).then_inc(hi_done, 1)

            def pair_program(ph, prep):
                for s in range(STEPS):
                    if s + 1 < STEPS or prep:
                        exponentials(ph.pair, s + 1)
                    if s % SBANKS == 3 and s > SBANKS:
                        copy_outputs(ph, s // SBANKS - 1)
                    turned_hi(ph, s)
                    if s in OUT_JOBS:
                        out_job(ph, OUT_JOBS[s][0])
                    elif prep and s in PREP_JOBS:
                        prep_job(ph, PREP_JOBS[s][0])
                copy_outputs(ph, STEPS // SBANKS - 1)

            ph = setup_ph
            for n in range(NG):
                for k in range(KE):
                    copy(xT_hi[:, k, n * BANK:(n + 1) * BANK], slot_of(ph, ("xT", n, k))).then_inc(hi_done, 1)
            for n in range(NG):
                copy(kraw[:, BLK * n:BLK * n + BLK, :].rearrange("p t c -> p (t c)"), slot_of(ph, ("kv", n))).then_inc(act_freed, 1)
            for n in range(NG):
                for side in "BA":
                    copy(K_hi["AB".index(side)][:, n * BANK:(n + 1) * BANK], slot_of(ph, ("K", n, side))).then_inc(hi_done, 1)
            for name, _ in PREP_FIRST:
                if name == "wabs":
                    pass
                prep_job(ph, name)
            if "pad" in SETUP.at:
                prep_job(ph, "pad")
            copy(spare[:, 1:2], ones[:]).then_inc(o_copied, 1)
            exponentials(0, 0)
            with act.Fori(0, PAIRS - 1) as p:
                pair_program(loop_ph.of_pair(p), True)
            pair_program(last_ph, False)
            ph = tail_ph
            for name, _ in OUT_LAST:
                out_job(ph, name)
            for w, k, half in FFN_UP:
                c = IT // 2 * P
                copy(upT_hi[:, w, k, half * c:(half + 1) * c], slot_of(ph, (w, k, half))[:, 0:c]).then_inc(hi_done, 1)
            for _, i in FFN_DOWN:
                copy(downT_hi[:, 2 * i:2 * i + 2, :].rearrange("p t e -> p (t e)"), slot_of(ph, (2, i))).then_inc(hi_done, 1)

            def hidden_hi(j):
                n, it = divmod(j, IT)
                act.wait_ge(hid_done, j + 1)
                if n >= 2:
                    act.wait_ge(down_ready, 2 * (n - 1))
                copy(hid_hi[:, n % 2, it, :], hid[:, j % 2, :]).then_inc(hid_hi_done, 1)

            def out_gate(u):
                act.wait_ge(down_ready, u + 1)
                if u >= 2:
                    act.wait_ge(gated, u - 1)
                bank = s_ps[:, SBANKS - 1, :] if u % 2 else o_ps[:, :]
                nc.scalar.activation(gate[:, u % 2].rearrange("p t e -> p (t e)"), bank, ACT.Silu).then_inc(gate_done, 1)

            for j in range(NG * IT):
                act.wait_ge(gu_ready, j + 1)
                if j >= 2:
                    act.wait_ge(hid_done, j - 1)
                nc.scalar.activation(silu_g[:, j % 2, :], s_ps[:, 2 * (j % 2), :], ACT.Silu).then_inc(silu_done, 1)
                if j >= 1:
                    hidden_hi(j - 1)
                if j % IT == 3 and j >= 2 * IT:
                    out_gate(2 * (j // IT) - 4)
                    out_gate(2 * (j // IT) - 3)
            hidden_hi(NG * IT - 1)
            for u in range(2 * NG - 4, 2 * NG):
                out_gate(u)

        @block.vector
        def _(dve):
            steps = [0]

            def then_wait(instruction):
                steps[0] += 1
                instruction.then_inc(dve_setup, 1)
                dve.wait_ge(dve_setup, steps[0])

            def lo_of(ph, name, dst, hi, cols=slice(0, BANK)):
                dve.wait_ge(hi_done, ph.after("hi", name))
                ps = slot_ps[:, ph.slots.at[name] % 2, cols]
                nc.vector.tensor_tensor(dst, ps, hi, ALU.subtract).then_inc(dve_freed, 1)

            def f32(ap):
                return ap.bitcast(F32)

            def out_job(ph, name):
                if name == "wvo":
                    lo_of(ph, name, wvo_lo[:], f32(wvo_hi[:]), slice(0, E))
                    return
                q = int(name[4])
                if name.startswith("outT"):
                    lo_of(ph, name, oT_lo[:, q % 2, :], f32(oT_hi[:, q % 2, :]))
                    return
                half = "ab".index(name[5])
                high, low = TILE_ORDER[4 * q + 2 * half:4 * q + 2 * half + 2]
                tiles = acc[:, low:high + 1:high - low, :]
                dve.wait_ge(slot_ready, ph.after("ready", name))
                ps = slot_ps[:, ph.slots.at[name] % 2, :].rearrange("p (t e) -> p t e", t=2)
                nc.vector.tensor_tensor(tiles, ps, tiles, ALU.add).then_inc(dve_freed, 1)

            def row_max(pair, g):
                _, _, tile_no, k0, w, first, last_chunk = chunk(g)
                pair = pair + g // STEPS
                g %= STEPS
                r = tile_no % TILE_RING
                c = k0 // BANK
                dve.wait_ge(scores_ready, pair * STEPS + g + 1)
                src = s_ps[:, g % SBANKS, 0:w]
                if first and last_chunk:
                    nc.vector.tensor_reduce(neg_max[:, r:r + 1], src, AX.X, ALU.max, negate=True).then_inc(max_ready, 1)
                    return
                nc.vector.tensor_reduce(part_max[:, r, c:c + 1], src, AX.X, ALU.max).then_inc(part_done, 1)
                if last_chunk:
                    dve.wait_ge(part_done, pair * PARTS + part_of[g])
                    nc.vector.tensor_reduce(neg_max[:, r:r + 1], part_max[:, r, 0:c + 1], AX.X, ALU.max, negate=True).then_inc(max_ready, 1)

            def normalise(ph, r):
                head, high = chunk(SBANKS * r)[:2]
                low = NT - 1 - high
                b = r % 2
                done = ph.pair * NT + r + 1
                dve.wait_ge(o_copied, 1 + done)
                nc.vector.tensor_tensor(o_sum[:, b], o_raw[:, b, :, 0:LORA], o_raw[:, b, :, LORA + 1:VW], ALU.add)
                nc.vector.reciprocal(rinv[:, b, :], o_raw[:, b, :, LORA]).then_inc(summed, 1)
                dve.wait_ge(summed, done)
                nc.vector.tensor_tensor(o_pair[:, high:(low - 1 if low else None):low - high, head * LORA:(head + 1) * LORA], o_sum[:, b],
                                        rinv[:, b, :].unsqueeze(2).to_broadcast([P, 2, LORA]), ALU.mult).then_inc(norm_done, 1)

            def pair_program(ph, prep):
                for s in range(STEPS):
                    w = chunk(s)[4]
                    if True:
                        lo_of(ph, ("T", s), pT_lo[:, s % PT_RING, 0:w], pT_hi[:, s % PT_RING, 0:w], slice(0, w))
                    if s + SBANKS < STEPS or prep:
                        row_max(ph.pair, s + SBANKS)
                    if False:
                        lo_of(ph, ("T", s), pT_lo[:, s % PT_RING, 0:w], pT_hi[:, s % PT_RING, 0:w], slice(0, w))
                    if s in OUT_JOBS:
                        out_job(ph, OUT_JOBS[s][0])
                    elif prep and s in PREP_JOBS and PREP_JOBS[s][0] == "wabs":
                        lo_of(ph, "wabs", wabs_lo[:].rearrange("p k c -> p (k c)"), f32(wabs_hi[:].rearrange("p k c -> p (k c)")), slice(0, KE * P))
                    if s % SBANKS == 3 and s > SBANKS:
                        normalise(ph, s // SBANKS - 1)
                normalise(ph, STEPS // SBANKS - 1)

            def stats(n):
                dve.wait_ge(x_loaded[n], 16)
                for t in range(BLK * n, BLK * n + BLK):
                    last = nc.vector.bn_stats(stat[:, t, :], acc[:, t, :])
                then_wait(last)
                for t in range(BLK * n, BLK * n + BLK):
                    last = nc.vector.bn_aggr(mv[:, t, :], stat[:, t, :])
                then_wait(last)
                then_wait(nc.vector.tensor_scalar(var_eps[:, BLK * n:BLK * n + BLK], mv[:, BLK * n:BLK * n + BLK, 1], EPS_LN, None, ALU.add))

            ph = setup_ph
            stats(0)
            nc.vector.memset(wvT[:], 0.0)
            then_wait(nc.vector.memset(wkvs[:], 0.0))
            nc.vector.memset(v[:], 1.0)
            for n in range(NG):
                if n + 1 < NG:
                    stats(n + 1)
                dve.wait_ge(pool_done, ph.pool_after(f"rstd{n}"))
                for t in range(BLK * n, BLK * n + BLK):
                    nc.vector.tensor_scalar(acc[:, t, :], acc[:, t, :], mv[:, t, 0:1], rstd[:, t:t + 1],
                                            ALU.subtract, ALU.mult).then_inc(xn_done, 1)
            dve.wait_ge(consts_loaded, 64)
            nc.vector.tensor_copy(wkva_hi[:], wkva_sb[:]).then_inc(wkva_done, 1)
            dve.wait_ge(wkva_done, 1)
            nc.vector.tensor_tensor(wkva_lo[:], wkva_sb[:], f32(wkva_hi[:]), ALU.subtract).then_inc(wkva_done, 1)
            for n in range(NG):
                for k in range(KE):
                    c = slice(n * BANK, (n + 1) * BANK)
                    lo_of(ph, ("xT", n, k), xT_lo[:, k, c], f32(xT_hi[:, k, c]))

            def squares(n):
                tiles = slice(BLK * n, BLK * n + BLK)
                ckv = kraw[:, tiles, 0:LORA]
                dve.wait_ge(act_freed, ph.after("act", ("kv", n)))
                then_wait(nc.vector.tensor_tensor(sq[:], ckv, ckv, ALU.mult))
                then_wait(nc.vector.tensor_reduce(ss[:, tiles], sq[:], AX.X, ALU.add))
                then_wait(nc.vector.tensor_scalar(ms_eps[:, tiles], ss[:, tiles], 1.0 / LORA, EPS_RMS, ALU.mult, ALU.add))

            def values_and_keys(n):
                tiles = slice(BLK * n, BLK * n + BLK)
                dve.wait_ge(pool_done, ph.pool_after(f"rms{n}"))
                then_wait(nc.vector.tensor_tensor(kn[:, tiles, :], kraw[:, tiles, 0:LORA],
                                                  rms[:, tiles].unsqueeze(2).to_broadcast([P, BLK, LORA]), ALU.mult))
                then_wait(nc.vector.tensor_copy(v[:, tiles, 0:LORA], kn[:, tiles, :]))
                nc.vector.tensor_tensor(v[:, tiles, LORA + 1:VW], kn[:, tiles, :], v[:, tiles, 0:LORA], ALU.subtract)
                nc.vector.tensor_scalar(kcat[:, tiles, 0:LORA], kn[:, tiles, :], SCALE, None, ALU.mult)
                nc.vector.tensor_scalar(kcat[:, tiles, 2 * LORA:3 * LORA], kn[:, tiles, :], SCALE, None, ALU.mult).then_inc(kcat_done, 1)

            squares(0)
            for n in range(NG):
                if n + 1 < NG:
                    squares(n + 1)
                values_and_keys(n)
            for n in range(NG):
                for side in "BA":
                    c = slice(n * BANK, (n + 1) * BANK)
                    i = "AB".index(side)
                    lo_of(ph, ("K", n, side), K_lo[i][:, c], f32(K_hi[i][:, c]))
            nc.vector.memset(acc[:], 0.0)
            nc.vector.memset(f32(wvo_hi[:]), 0.0)
            nc.vector.memset(f32(wvo_lo[:]), 0.0)
            nc.vector.memset(o_pair[:], 0.0).then_inc(norm_done, 1)
            lo_of(ph, "wabs", wabs_lo[:].rearrange("p k c -> p (k c)"), f32(wabs_hi[:].rearrange("p k c -> p (k c)")), slice(0, KE * P))
            for g in range(SBANKS):
                row_max(0, g)
            with dve.Fori(0, PAIRS - 1) as p:
                pair_program(loop_ph.of_pair(p), True)
            pair_program(last_ph, False)
            ph = tail_ph
            for name, _ in OUT_LAST:
                out_job(ph, name)

            nc.vector.memset(up_raw[:, :, IT - 1, :], 0.0)
            nc.vector.memset(up_scale[:], 0.0)
            nc.vector.memset(down_raw[:, :, INTER:IT * P], 0.0).then_inc(ffn_zero, 1)
            dve.wait_ge(ffn_loaded, 16 * 10)
            for w in range(2):
                nc.vector.tensor_tensor(up_raw[:, w], up_raw[:, w], up_scale[:, w, :].unsqueeze(2).to_broadcast([P, IT, E]), ALU.mult).then_inc(ffn_scaled, 1)
            for k in range(KE):
                nc.vector.tensor_scalar(down_raw[:, k, :], down_raw[:, k, :], down_scale[:, k:k + 1], None, ALU.mult).then_inc(ffn_scaled, 1)
            for w, k, half in FFN_UP:
                c = slice(half * (IT // 2 * P), (half + 1) * (IT // 2 * P))
                lo_of(ph, (w, k, half), upT_lo[:, w, k, c], f32(upT_hi[:, w, k, c]), slice(0, IT // 2 * P))
            for _, i in FFN_DOWN:
                lo_of(ph, (2, i), downT_lo[:, 2 * i:2 * i + 2, :].rearrange("p t e -> p (t e)"),
                      f32(downT_hi[:, 2 * i:2 * i + 2, :].rearrange("p t e -> p (t e)")))

            def finish(u):
                tiles = slice(2 * u, 2 * u + 2)
                dve.wait_ge(gate_done, u + 1)
                if u >= 2:
                    dve.wait_ge(stored[u % 2], 16 * (u // 2))
                nc.vector.tensor_tensor(y[:, u % 2], gate[:, u % 2], acc[:, tiles, :], ALU.mult).then_inc(gated, 1)
                dve.wait_ge(gated, u + 1)
                if u == 0:
                    dve.wait_ge(x_again, 16)
                nc.vector.tensor_tensor(y[:, u % 2], y[:, u % 2], x_in[:, tiles, :], ALU.add).then_inc(y_done, 1)

            for j in range(NG * IT):
                dve.wait_ge(silu_done, j + 1)
                if j >= 2:
                    dve.wait_ge(hid_lo_done, j - 1)
                nc.vector.tensor_tensor(hid[:, j % 2, :], s_ps[:, 2 * (j % 2) + 1, :], silu_g[:, j % 2, :], ALU.mult).then_inc(hid_done, 1)
                if j % IT == 4 and j >= 2 * IT:
                    finish(2 * (j // IT) - 4)
                    finish(2 * (j // IT) - 3)
            for u in range(2 * NG - 4, 2 * NG):
                finish(u)

        @block.gpsimd
        def _(pool):
            def run(ph, name, issue, *waits):
                value = ph.pool_after(name)
                if ph is not setup_ph or ph.pool.after[name] > 1:
                    pool.wait_ge(pool_done, value - 1)
                for s, v in waits:
                    pool.wait_ge(s, v)
                issue().then_inc(pool_done, 1)

            def tt(dst, a, b, op):
                return lambda: nc.gpsimd.tensor_tensor(dst, a, b, op)

            def split_queries(ph, head, *waits):
                h = "qa" if head == 0 else "qb"
                lat_rows = slice(LORA, P) if head == 0 else slice(0, LORA)
                pe_rows = slice(0, LORA) if head == 0 else slice(LORA, P)
                for what, src, rows in (("lat", lat, lat_rows), ("pe", pe, pe_rows)):
                    run(ph, f"{h}_{what}_hi", tt(Q_hi[head][rows, :], src[rows, :], ones[rows, :].to_broadcast([LORA, S]), ALU.mult), *waits)
                    run(ph, f"{h}_{what}_lo", tt(Q_lo[head][rows, :], src[rows, :], Q_hi[head][rows, :].bitcast(F32), ALU.subtract))
                    waits = ()

            def weights(ph, pairs):
                free = () if ph is setup_ph else ((slot_ready, ph.base["ready"]),)
                pew = wq_sb[:].rearrange("p k (h c) -> p k h c", h=2)[:, :, :, NOPE:NOPE + ROPE]
                run(ph, "wpe_hi", tt(wpe_hi[:], pew, ones[:].unsqueeze(2).unsqueeze(3).to_broadcast([P, KE, 2, ROPE]), ALU.mult), (wq_loaded, 16 * pairs), *free)
                run(ph, "wpe_lo", tt(wpe_lo[:], pew, wpe_hi[:].bitcast(F32), ALU.subtract))
                run(ph, "wkvs", tt(wkvs[0:LORA, :], wkv_sb[:], scale_sb[:].to_broadcast([LORA, KVW]), ALU.mult),
                    (wkv_loaded, 16 * pairs), (consts_loaded, 64), (dve_setup, 4))

            def rotate(ph, step, src, dst, c_buf, s_buf, n, parts, *waits):
                half = ROPE // 2
                tiles = slice(BLK * n, BLK * n + BLK)

                def table(tab, m):
                    return tab[:, tiles, :].unsqueeze(2).to_broadcast([P, BLK, m, half])

                def halves(ap, i):
                    return ap.rearrange("p t (m x d) -> p t m x d", m=parts, x=2)[:, :, :, i, :]

                whole = lambda ap: ap.rearrange("p t (m d) -> p t m d", d=half)
                run(ph, step(0), tt(whole(c_buf), whole(src), table(cos_sb, 2 * parts), ALU.mult), *waits)
                run(ph, step(1), tt(halves(s_buf, 0), halves(src, 1), table(sin_sb, parts), ALU.mult))
                run(ph, step(2), tt(halves(s_buf, 1), halves(src, 0), table(sin_sb, parts), ALU.mult))
                run(ph, step(3), tt(halves(dst, 0), halves(c_buf, 0), halves(s_buf, 0), ALU.subtract))
                run(ph, step(4), tt(halves(dst, 1), halves(c_buf, 1), halves(s_buf, 1), ALU.add))

            def rotate_queries(ph):
                for n in range(NG):
                    waits = [(act_freed, ph.after("act", f"pe{n}"))]
                    if n >= 2:
                        waits.append((slot_ready, ph.after("ready", f"peT{n - 2}")))
                    rotate(ph, lambda i: f"rope{n}.{i}", qtok[:, n % 2], qrot[:, n % 2], rope_c[:], rope_s[:], n, 2, *waits)

            ph = setup_ph
            run(ph, "half", lambda: nc.gpsimd.memset(minus_half[:], -0.5))
            run(ph, "ones", lambda: nc.gpsimd.memset(ones[:], 1.0))
            run(ph, "ident0", lambda: nc.gpsimd.memset(ident[:], 0.0))
            run(ph, "ident", lambda: nc.gpsimd.affine_select(out=ident[:], in_=ident[:], compare_op=ALU.not_equal, fill=1.0,
                                                             base=0, pattern=[[-1, P]], channel_multiplier=1))
            for n in range(NG):
                c = slice(BLK * n, BLK * n + BLK)
                run(ph, f"rstd{n}", tt(rstd[:, c], var_eps[:, c], minus_half[:], ALU.pow), (dve_setup, 3 * (n + 1) + (n > 0)))
            run(ph, "identb", lambda: nc.gpsimd.tensor_copy(identb[:], ident[:]))
            run(ph, "mask0", lambda: nc.gpsimd.memset(mask[:], 0.0))
            run(ph, "mask", lambda: nc.gpsimd.affine_select(out=mask[:], in_=mask[:], compare_op=ALU.is_ge, fill=MASKED,
                                                            base=0, pattern=[[-1, P]], channel_multiplier=1))
            for n in range(NG):
                c = slice(BLK * n, BLK * n + BLK)
                step = 3 * NG + 1 + 3 * (n + 1) + 2 * max(n - 1, 0)
                run(ph, f"rms{n}", tt(rms[:, c], ms_eps[:, c], minus_half[:], ALU.pow), (dve_setup, step))
                rotate(ph, lambda i: f"kr{n}.{i}", kraw[:, c, LORA:P], krot[:, c, :], krope_c[:, c, :], krope_s[:, c, :], n, 1,
                       (act_freed, ph.after("act", ("kv", n))), (consts_loaded, 64))
                run(ph, f"kr{n}.5", lambda: nc.gpsimd.tensor_scalar(kcat[:, c, LORA:2 * LORA], krot[:, c, :], SCALE, 1.0, ALU.mult, ALU.mult))
            weights(ph, 1)
            rotate_queries(ph)
            split_queries(ph, 0, (act_freed, ph.after("act", "lat3")), (act_freed, ph.after("act", "peT3")))
            with pool.Fori(0, PAIRS - 1) as p:
                ph = loop_ph.of_pair(p)
                split_queries(ph, 1, (scores_ready, p * STEPS + SBANKS), (act_freed, ph.base["act"]))
                weights(ph, p + 2)
                rotate_queries(ph)
                split_queries(ph, 0, (act_freed, ph.after("act", "lat3")), (act_freed, ph.after("act", "peT3")),
                              (scores_ready, p * STEPS + NCH))
            split_queries(last_ph, 1, (scores_ready, (PAIRS - 1) * STEPS + SBANKS), (act_freed, last_ph.base["act"]))

            for j in range(NG * IT):
                n, it = divmod(j, IT)
                pool.wait_ge(hid_hi_done, j + 1)
                nc.gpsimd.tensor_tensor(hid_lo[:, n % 2, it, :], hid[:, j % 2, :], hid_hi[:, n % 2, it, :].bitcast(F32), ALU.subtract).then_inc(hid_lo_done, 1)


_INS = ["L0_attn_x", "L0_attn_wq", "L0_attn_wkv_a", "L0_attn_wkv_b", "L0_attn_wo", "L0_attn_kv_norm_scale",
        "L0_ffn_gate_w", "L0_ffn_up_w", "L0_ffn_down_w", "L0_ffn_gate_s", "L0_ffn_up_s", "L0_ffn_down_s"]


def kernel(**inputs):
    import numpy as _np
    import concourse.bacc as _bacc
    from concourse import mybir as _mybir
    from concourse.bass_utils import run_bass_kernel_spmd as _run

    nc = _bacc.Bacc("TRN2", target_bir_lowering=False, num_devices=1)
    inv = (1.0 / _np.float32(10000.0) ** (_np.arange(0, ROPE, 2, dtype=_np.float32) / _np.float32(ROPE))).astype(_np.float32)
    angle = _np.arange(S, dtype=_np.float32)[:, None] * inv
    arrays = {"cos_dram": _np.cos(angle.astype(_np.float64)).astype(_np.float32),
              "sin_dram": _np.sin(angle.astype(_np.float64)).astype(_np.float32)}
    args = []
    for name in _INS:
        a = _np.ascontiguousarray(inputs[name])
        arrays[f"in_{name}_dram"] = a
        args.append(nc.dram_tensor(f"in_{name}_dram", a.shape, _mybir.dt.from_np(a.dtype), kind="ExternalInput").ap())
    for name in ("cos_dram", "sin_dram"):
        args.append(nc.dram_tensor(name, (S, ROPE // 2), F32, kind="ExternalInput").ap())
    args.append(nc.dram_tensor("out_0_dram", (1, S, E), F32, kind="ExternalOutput").ap())
    mla_gated_ffn_kernel(nc, *args)
    r = _run(nc, [arrays], core_ids=[0])
    return r.results[0]["out_0_dram"]
```

```python
from contextlib import ExitStack

import concourse.bass as bass
import concourse.mybir as mybir

F32 = mybir.dt.float32
F32R = mybir.dt.float32r
F16 = mybir.dt.float16
BF16 = mybir.dt.bfloat16
ALU = mybir.AluOpType
ACT = mybir.ActivationFunctionType
AX = mybir.AxisListType

P = 128
S, E = 2048, 256
H, NOPE, ROPE, VD, LORA = 16, 128, 64, 128, 64
INTER = 704
EPS_LN, EPS_RMS = 1e-5, 1e-6
SCALE = float((NOPE + ROPE) ** -0.5)
MASKED = -3.0e38
NT = S // P
KE = E // P
BANK = 512
BLK = BANK // P
NG = NT // BLK
PAIRS = H // 2
QW = 2 * (NOPE + ROPE)
KVW = 2 * (NOPE + VD)
IT = -(-INTER // P)
SBANKS = 5
NP_RING, PT_RING, TILE_RING = 4, 5, 4
VW = 2 * LORA + 1

TILE_ORDER = [t for k in range(NT // 2) for t in (NT - 1 - k, k)]
CHUNKS = []
for pos, t in enumerate(TILE_ORDER):
    keys = (t + 1) * P
    for k0 in range(0, keys, BANK):
        CHUNKS.append((t, pos, k0, min(BANK, keys - k0), k0 == 0, k0 + BANK >= keys))
NCH = len(CHUNKS)
STEPS = 2 * NCH


WEIGH = {0: (-3,), 1: (-3,), 2: (-3,), 3: (), 4: (-4, -3)}


def weigh_at(step):
    return [step + d for d in WEIGH[step % SBANKS] if step + d >= 0]


WEIGH_END = range(STEPS - 3, STEPS)


def chunk(g):
    g %= STEPS
    t, pos, k0, w, first, last = CHUNKS[g % NCH]
    head = g // NCH
    return head, t, head * NT + pos, k0, w, first, last


class Slots:

    def __init__(self):
        self.kinds, self.counts, self.at = [], [], {}
        self.count = {"ready": 0, "hi": 0, "act": 0, "dve": 0}

    def add(self, name, kind):
        self.count["ready"] += 1
        if kind == "split":
            self.count["hi"] += 1
        self.count["act" if kind == "act" else "dve"] += 1
        self.kinds.append(kind)
        self.counts.append(dict(self.count))
        self.at[name] = len(self.kinds) - 1


class Phase:

    def __init__(self, slots, pool, base, pool_base, pair=None):
        self.slots, self.pool, self.base, self.pool_base, self.pair = slots, pool, base, pool_base, pair

    def of_pair(self, pair):
        base = {k: self.base[k] + pair * self.slots.count[k] for k in self.base}
        return Phase(self.slots, self.pool, base, self.pool_base + pair * len(self.pool.names), pair)

    def after(self, kind, name):
        return self.base[kind] + self.slots.counts[self.slots.at[name]][kind]

    def pool_after(self, name):
        return self.pool_base + self.pool.after[name]

    def end(self, times=1):
        return {k: self.base[k] + times * self.slots.count[k] for k in self.base}


SPLIT, BY_ACT, BY_DVE = "split", "act", "dve"

OUT_JOBS = {1: ("outT3", SPLIT), 3: ("outP3a", BY_DVE), 5: ("outP3b", BY_DVE), 8: ("wvo", SPLIT),
            56: ("outT0", SPLIT), 58: ("outP0a", BY_DVE), 60: ("outP0b", BY_DVE),
            66: ("outT1", SPLIT), 68: ("outP1a", BY_DVE), 70: ("outP1b", BY_DVE),
            75: ("outT2", SPLIT), 77: ("outP2a", BY_DVE), 79: ("outP2b", BY_DVE)}
PREP_JOBS = {11: ("wqT", BY_ACT), 14: ("wkvT", BY_ACT), 16: ("pe0", BY_ACT), 18: ("wabs", SPLIT), 20: ("pe1", BY_ACT),
             22: ("lat0", BY_ACT), 24: ("pe2", BY_ACT), 26: ("peT0", BY_ACT), 28: ("lat1", BY_ACT),
             30: ("pe3", BY_ACT), 32: ("peT1", BY_ACT), 34: ("lat2", BY_ACT), 37: ("peT2", BY_ACT),
             39: ("lat3", BY_ACT), 42: ("peT3", BY_ACT)}
FFN_UP = [(w, k, half) for w in range(2) for k in range(KE) for half in range(2)]
FFN_DOWN = [(2, i) for i in range(IT // 2)]
FFN_JOBS = {s: (name, SPLIT) for s, name in zip((40, 42, 44, 46, 48, 50, 52, 54, 62, 64, 72), FFN_UP + FFN_DOWN)}
LOOP_JOBS, LAST_JOBS = {**OUT_JOBS, **PREP_JOBS}, {**OUT_JOBS, **FFN_JOBS}
OUT_LAST = [OUT_JOBS[s] for s in (1, 3, 5)]
PREP_FIRST = [("wqT", BY_ACT), ("pe0", BY_ACT), ("wkvT", BY_ACT), ("pe1", BY_ACT), ("wabs", SPLIT),
              ("pe2", BY_ACT), ("peT0", BY_ACT), ("pe3", BY_ACT), ("lat0", BY_ACT), ("peT1", BY_ACT),
              ("lat1", BY_ACT), ("peT2", BY_ACT), ("lat2", BY_ACT), ("peT3", BY_ACT), ("lat3", BY_ACT)]


def pair_slots(jobs):
    slots = Slots()
    for s in range(STEPS):
        slots.add(("T", s), SPLIT)
        if s in jobs:
            slots.add(*jobs[s])
    return slots


SETUP = Slots()
for n in range(NG):
    for k in range(KE):
        SETUP.add(("xT", n, k), SPLIT)
for n in range(NG):
    SETUP.add(("kv", n), BY_ACT)
for n in range(NG):
    for side in "BA":
        SETUP.add(("K", n, side), SPLIT)
for name, kind in PREP_FIRST:
    SETUP.add(name, kind)
if len(SETUP.kinds) % 2:
    SETUP.add("pad", BY_ACT)
LOOP, LAST = pair_slots(LOOP_JOBS), pair_slots(LAST_JOBS)
assert len(LOOP.kinds) % 2 == 0
TAIL = Slots()
for name, kind in OUT_LAST:
    TAIL.add(name, kind)

POOL_SETUP = ["half", "ones", "ident0", "ident"] + [f"rstd{n}" for n in range(NG)] + ["identb", "mask0", "mask"] + [
    x for n in range(NG) for x in [f"rms{n}"] + [f"kr{n}.{i}" for i in range(6)]]
POOL_W = ["wpe_hi", "wpe_lo", "wkvs"]
POOL_QB = ["qb_lat_hi", "qb_lat_lo", "qb_pe_hi", "qb_pe_lo"]
POOL_ROPE = [f"rope{n}.{i}" for n in range(NG) for i in range(5)]
POOL_QA = ["qa_lat_hi", "qa_lat_lo", "qa_pe_hi", "qa_pe_lo"]


class Steps:

    def __init__(self, names):
        self.names = names
        self.after = {n: i + 1 for i, n in enumerate(names)}


POOL_PRO = Steps(POOL_SETUP + POOL_W + POOL_ROPE + POOL_QA)
POOL_LOOP = Steps(POOL_QB + POOL_W + POOL_ROPE + POOL_QA)
POOL_LAST = Steps(POOL_QB + ["up_zero", "up_scale_zero", "down_zero", "up_scaled0", "up_scaled1", "down_scaled"])


def mla_gated_ffn_kernel(nc, x, wq, wkv_a, wkv_b, wo, kv_scale, gate_w, up_w, down_w, gate_s, up_s,
                         down_s, cos_in, sin_in, out):
    with ExitStack() as ctx:
        def sem(name):
            return ctx.enter_context(nc.semaphore(name))

        def sb(name, shape, dt=F32, where=ctx):
            return where.enter_context(nc.sbuf_tensor(name, shape, dt))

        xT_hi = sb("xT_hi", [P, KE, S], F32R)
        xT_lo = sb("xT_lo", [P, KE, S], F32R)
        acc = sb("acc", [P, NT, E])
        ident = sb("ident", [P, P])

        setup = ExitStack()

        def ub(name, shape, dt=F32):
            return sb(name, shape, dt, setup)

        wkva_sb = ub("wkva_sb", [P, KE, P])
        wkva_hi = ub("wkva_hi", [P, KE, P], F32R)
        wkva_lo = ub("wkva_lo", [P, KE, P], F32R)
        kraw = ub("kraw", [P, NT, P])
        kcat = ub("kcat", [P, NT, 3 * LORA])
        kn = ub("kn", [P, NT, LORA])
        sq = ub("sq", [P, BLK, LORA])
        krope_c = ub("krope_c", [P, NT, ROPE])
        krope_s = ub("krope_s", [P, NT, ROPE])
        krot = ub("krot", [P, NT, ROPE])
        stat = ub("stat", [P, NT, 6])
        mv = ub("mv", [P, NT, 2])
        var_eps = ub("var_eps", [P, NT])
        minus_half = ub("minus_half", [P, BLK])
        rstd = ub("rstd", [P, NT])
        ss = ub("ss", [P, NT])
        ms_eps = ub("ms_eps", [P, NT])
        rms = ub("rms", [P, NT])
        setup.close()

        attn = ExitStack()

        def ab(name, shape, dt=F32):
            return sb(name, shape, dt, attn)

        lat = ab("lat", [P, S])
        pe = ab("pe", [P, S])
        qtok = ab("qtok", [P, 2, BLK, P])
        qrot = ab("qrot", [P, 2, BLK, P])
        rope_c = ab("rope_c", [P, BLK, P])
        rope_s = ab("rope_s", [P, BLK, P])
        QA_hi, QA_lo = ab("QA_hi", [P, S], F32R), ab("QA_lo", [P, S], F32R)
        wq_sb = ab("wq_sb", [P, KE, QW])
        wpe_hi = ab("wpe_hi", [P, KE, 2, ROPE], F32R)
        wpe_lo = ab("wpe_lo", [P, KE, 2, ROPE], F32R)
        wqT = ab("wqT", [P, 2, KE, P])
        wkv_sb = ab("wkv_sb", [LORA, KVW])
        wkvs = ab("wkvs", [P, KVW])
        wkT = ab("wkT", [P, 2, LORA])
        QB_hi, QB_lo = ab("QB_hi", [P, S], F32R), ab("QB_lo", [P, S], F32R)
        Q_hi, Q_lo = [QA_hi, QB_hi], [QA_lo, QB_lo]
        K_hi = [ab(f"K{h}_hi", [P, S], F32R) for h in "AB"]
        K_lo = [ab(f"K{h}_lo", [P, S], F32R) for h in "AB"]
        prob = ab("prob", [P, NP_RING, BANK])
        pT_hi = ab("pT_hi", [P, PT_RING, BANK], F16)
        pT_lo = ab("pT_lo", [P, PT_RING, BANK], F16)
        o_raw = ab("o_raw", [P, 2, 2, VW])
        o_sum = ab("o_sum", [P, 2, 2, LORA])
        o_pair = ab("o_pair", [P, NT, P])
        oT_hi = ab("oT_hi", [P, 2, BANK], F32R)
        oT_lo = ab("oT_lo", [P, 2, BANK], F32R)
        v = ab("v", [P, NT, VW + 1], F16)
        ones = ab("ones", [P, 1])
        spare = ab("spare", [P, 2])
        wvT = ab("wvT", [P, 2, P])
        wo_sb = ab("wo_sb", [P, 2, E])
        wabs_hi = ab("wabs_hi", [P, KE, P], F32R)
        wabs_lo = ab("wabs_lo", [P, KE, P], F32R)
        wvo_hi = ab("wvo_hi", [P, E], F32R)
        wvo_lo = ab("wvo_lo", [P, E], F32R)
        cos_sb = ab("cos_sb", [P, NT, ROPE // 2])
        sin_sb = ab("sin_sb", [P, NT, ROPE // 2])
        scale_sb = ab("scale_sb", [LORA, 1])
        mask = ab("mask", [P, P], BF16)
        identb = ab("identb", [P, P], BF16)
        part_max = ab("part_max", [P, TILE_RING, BLK])
        neg_max = ab("neg_max", [P, TILE_RING])
        rinv = ab("rinv", [P, 2, 2])
        attn.close()

        ffn = ExitStack()

        def fb(name, shape, dt=F32):
            return sb(name, shape, dt, ffn)

        up_raw = fb("up_raw", [P, 2, IT, E])
        down_raw = fb("down_raw", [P, KE, IT * P])
        up_scale = fb("up_scale", [P, 2, IT])
        down_scale = fb("down_scale", [P, KE])
        upT_hi = fb("upT_hi", [P, 2, KE, IT * P], F32R)
        upT_lo = fb("upT_lo", [P, 2, KE, IT * P], F32R)
        downT_hi = fb("downT_hi", [P, IT, E], F32R)
        downT_lo = fb("downT_lo", [P, IT, E], F32R)
        silu_g = fb("silu_g", [P, 2, BANK])
        hid = fb("hid", [P, 2, BANK])
        hid_hi = fb("hid_hi", [P, 2, IT, BANK], F32R)
        x_in = fb("x_in", [P, NT, E])
        hid_lo = fb("hid_lo", [P, 2, IT, BANK], F32R)
        gate = fb("gate", [P, 2, 2, E])
        y = fb("y", [P, 2, 2, E])
        ffn.close()

        s_ps = ctx.enter_context(nc.psum_tensor("s_ps", [P, SBANKS, BANK], F32))
        slot_ps = ctx.enter_context(nc.psum_tensor("slot_ps", [P, 2, BANK], F32))
        o_ps = ctx.enter_context(nc.psum_tensor("o_ps", [P, BANK], F32))

        x_loaded = [sem(f"x_loaded{n}") for n in range(NG)]
        consts_loaded = sem("consts_loaded")
        wq_loaded, wkv_loaded, wo_loaded = sem("wq_loaded"), sem("wkv_loaded"), sem("wo_loaded")
        slot_ready, hi_done = sem("slot_ready"), sem("hi_done")
        act_freed, dve_freed = sem("act_freed"), sem("dve_freed")
        pool_done = sem("pool_done")
        dve_setup = sem("dve_setup")
        xn_done = sem("xn_done")
        kcat_done = sem("kcat_done")
        wkva_done = sem("wkva_done")
        scores_ready = sem("scores_ready")
        part_done = sem("part_done")
        max_ready = sem("max_ready")
        exp_done = sem("exp_done")
        pv_done = sem("pv_done")

        o_copied = sem("o_copied")
        summed = sem("summed")
        norm_done = sem("norm_done")
        ffn_loaded = sem("ffn_loaded")
        gu_ready, silu_done, hid_done = sem("gu_ready"), sem("silu_done"), sem("hid_done")
        hid_hi_done, hid_lo_done = sem("hid_hi_done"), sem("hid_lo_done")
        down_ready, gate_done = sem("down_ready"), sem("gate_done")
        gated, y_done = sem("gated"), sem("y_done")
        stored = [sem("stored0"), sem("stored1")]
        x_again = sem("x_again")

        setup_ph = Phase(SETUP, POOL_PRO, {"ready": 0, "hi": 0, "act": 0, "dve": 0}, 0)
        loop_ph = Phase(LOOP, POOL_LOOP, setup_ph.end(), len(POOL_PRO.names))
        last_ph = Phase(LAST, POOL_LAST, loop_ph.end(PAIRS - 1),
                        loop_ph.pool_base + (PAIRS - 1) * len(POOL_LOOP.names), PAIRS - 1)
        tail_ph = Phase(TAIL, None, last_ph.end(), 0)
        PARTS = sum(not (c[4] and c[5]) for c in CHUNKS) * 2
        part_of = {}
        for g in range(STEPS):
            first, last = chunk(g)[5:]
            part_of[g] = len([i for i in part_of.values() if i]) + 1 if not (first and last) else 0

        block = ctx.enter_context(nc.Block())

        @block.sync
        def _(sp):
            xv = x[0].rearrange("(t p) d -> p t d", p=P)
            for n in range(NG):
                sp.dma_start(acc[:, BLK * n:BLK * n + BLK, :], xv[:, BLK * n:BLK * n + BLK, :]).then_inc(x_loaded[n], 16)
            sp.dma_start(wkva_sb[:], wkv_a.rearrange("(k e) c -> e k c", k=KE)).then_inc(consts_loaded, 16)
            sp.dma_start(cos_sb[:], cos_in.rearrange("(t p) d -> p t d", p=P)).then_inc(consts_loaded, 16)
            sp.dma_start(sin_sb[:], sin_in.rearrange("(t p) d -> p t d", p=P)).then_inc(consts_loaded, 16)
            sp.dma_start(scale_sb[:], kv_scale.rearrange("(l o) -> l o", o=1)).then_inc(consts_loaded, 16)

            def load(pair):
                wqv = wq.rearrange("(k e) n -> e k n", k=KE)
                sp.dma_start(wq_sb[:], wqv[:, :, bass.ds(pair * QW, QW)]).then_inc(wq_loaded, 16)
                sp.dma_start(wkv_sb[:], wkv_b[:, bass.ds(pair * KVW, KVW)]).then_inc(wkv_loaded, 16)

            def load_wo(pair):
                wov = wo.rearrange("(h d) n -> d h n", d=VD)
                sp.dma_start(wo_sb[:], wov[:, bass.ds(pair * 2, 2), :]).then_inc(wo_loaded, 16)

            load(0)
            load_wo(0)
            with sp.Fori(0, PAIRS - 1) as p:
                ph = loop_ph.of_pair(p)
                sp.wait_ge(slot_ready, ph.base["ready"])
                sp.wait_ge(pool_done, ph.pool_base)
                load(p + 1)
                sp.wait_ge(slot_ready, ph.after("ready", "wvo"))
                load_wo(p + 1)

            sp.wait_ge(slot_ready, last_ph.base["ready"])
            sp.wait_ge(pool_done, last_ph.pool_after("down_zero"))
            whole = INTER // P
            rest = INTER - whole * P
            for w, src in enumerate((gate_w, up_w)):
                sp.dma_start(up_raw[:, w, 0:whole, :], src[0:whole * P, :].rearrange("(t p) e -> p t e", p=P)).then_inc(ffn_loaded, 16)
                sp.dma_start(up_raw[0:rest, w, whole, :], src[whole * P:INTER, :]).then_inc(ffn_loaded, 16)
            for w, src in enumerate((gate_s, up_s)):
                with nc.allow_non_contiguous_dma(reason="scales, one value to a partition"):
                    sp.dma_start(up_scale[:, w, 0:whole], src[0:whole * P].rearrange("(t p) -> p t", p=P)).then_inc(ffn_loaded, 16)
                    sp.dma_start(up_scale[0:rest, w, whole:whole + 1], src[whole * P:INTER].rearrange("(p o) -> p o", o=1)).then_inc(ffn_loaded, 16)
            sp.dma_start(down_raw[:, :, 0:INTER], down_w.rearrange("(k p) i -> p k i", p=P)).then_inc(ffn_loaded, 16)
            with nc.allow_non_contiguous_dma(reason="scales, one value to a partition"):
                sp.dma_start(down_scale[:], down_s.rearrange("(k p) -> p k", p=P)).then_inc(ffn_loaded, 16)
            sp.wait_ge(scores_ready, PAIRS * STEPS)
            sp.dma_start(x_in[:], xv).then_inc(x_again, 16)
            yv = out[0].rearrange("(t p) d -> p t d", p=P)
            for u in range(2 * NG):
                sp.wait_ge(y_done, u + 1)
                sp.dma_start(yv[:, 2 * u:2 * u + 2, :], y[:, u % 2]).then_inc(stored[u % 2], 16)
            for done in stored:
                sp.wait_ge(done, 16 * NG)

        @block.tensor
        def _(pe_eng):
            def slot(ph, name):
                i = ph.slots.at[name]
                if i >= 2:
                    freed = "act" if ph.slots.kinds[i - 2] == BY_ACT else "dve"
                    pe_eng.wait_ge(act_freed if freed == "act" else dve_freed,
                                   ph.base[freed] + ph.slots.counts[i - 2][freed])
                elif ph is not setup_ph and i == 0:
                    pe_eng.wait_ge(act_freed, ph.base["act"])
                    pe_eng.wait_ge(dve_freed, ph.base["dve"])
                return slot_ps[:, i % 2, :]

            def exact(out_ap, parts):
                n = 3 * len(parts)
                i = 0
                for a_hi, a_lo, b_hi, b_lo in parts:
                    for a, b in ((a_hi, b_hi), (a_hi, b_lo), (a_lo, b_hi)):
                        last = nc.tensor.matmul(out_ap, a, b, start=(i == 0), stop=(i == n - 1))
                        i += 1
                return last

            def x_tile(t):
                return [(xT_hi[:, k, t * P:(t + 1) * P], xT_lo[:, k, t * P:(t + 1) * P]) for k in range(KE)]

            def prep_job(ph, name, pair_after):
                ps = slot(ph, name)
                if name == "wqT":
                    pe_eng.wait_ge(wq_loaded, 16 * pair_after)
                    for h in range(2):
                        for k in range(KE):
                            c = h * (NOPE + ROPE)
                            last = nc.tensor.transpose(ps[:, (h * KE + k) * P:(h * KE + k + 1) * P], wq_sb[:, k, c:c + NOPE], ident[:])
                elif name == "wkvT":
                    pe_eng.wait_ge(pool_done, ph.pool_after("wkvs"))
                    for i in range(4):
                        last = nc.tensor.transpose(ps[:, i * P:(i + 1) * P], wkvs[:, i * P:(i + 1) * P], ident[:])
                elif name == "wabs":
                    pe_eng.wait_ge(act_freed, ph.after("act", "wkvT"))
                    for k in range(KE):
                        for h in (1, 0):
                            c = k * P + (1 - h) * LORA
                            last = nc.tensor.matmul(ps[:, c:c + LORA], wqT[:, h, k, :], wkT[:, h, :], start=True, stop=True)
                elif name.startswith("lat"):
                    n = int(name[3:])
                    pe_eng.wait_ge(dve_freed, ph.after("dve", "wabs"))
                    c = slice(n * BANK, (n + 1) * BANK)
                    last = exact(ps, [(wabs_hi[:, k, :], wabs_lo[:, k, :], xT_hi[:, k, c], xT_lo[:, k, c]) for k in range(KE)])
                elif name.startswith("peT"):
                    n = int(name[3:])
                    pe_eng.wait_ge(pool_done, ph.pool_after(f"rope{n}.4"))
                    for j in range(BLK):
                        last = nc.tensor.transpose(ps[:, j * P:(j + 1) * P], qrot[:, n % 2, j, :], ident[:])
                else:
                    n = int(name[2:])
                    pe_eng.wait_ge(pool_done, ph.pool_after("wpe_lo"))
                    for j in range(BLK):
                        w = [(wpe_hi[:, k, :, :].rearrange("p h c -> p (h c)"), wpe_lo[:, k, :, :].rearrange("p h c -> p (h c)")) for k in range(KE)]
                        last = exact(ps[:, j * P:(j + 1) * P], [(*a, *b) for a, b in zip(x_tile(BLK * n + j), w)])
                last.then_inc(slot_ready, 1)

            def out_job(ph, name, pair):
                if name == "wvo":
                    ps = slot(ph, name)
                    pe_eng.wait_ge(wo_loaded, 16 * (pair + 1))
                    for h in range(2):
                        last = nc.tensor.matmul(ps[:, 0:E], wvT[:, h, :], wo_sb[:, h, :], start=(h == 0), stop=(h == 1))
                    last.then_inc(slot_ready, 1)
                    return
                q = int(name[4])
                if name.startswith("outT"):
                    ps = slot(ph, name)
                    done = 1 + NT * pair if q == NG - 1 else 1 + NT * pair + NT // 2 + 2 * q + 2
                    pe_eng.wait_ge(norm_done, done)
                    for j in range(BLK):
                        last = nc.tensor.transpose(ps[:, j * P:(j + 1) * P], o_pair[:, TILE_ORDER[4 * q + j], :], ident[:])
                else:
                    half = "ab".index(name[5])
                    ps = slot(ph, name)
                    pe_eng.wait_ge(dve_freed, ph.after("dve", f"outT{q}"))
                    for i, j in enumerate((2 * half + 1, 2 * half)):
                        c = slice(j * P, (j + 1) * P)
                        last = exact(ps[:, i * E:(i + 1) * E], [(oT_hi[:, q % 2, c], oT_lo[:, q % 2, c], wvo_hi[:], wvo_lo[:])])
                last.then_inc(slot_ready, 1)

            def scores(g, queries_ready):
                head, t, _, k0, w, first, last_chunk = chunk(g)
                if g % NCH == 0:
                    pe_eng.wait_ge(pool_done, queries_ready)
                out_ap = s_ps[:, g % SBANKS, 0:w]
                q = slice(t * P, (t + 1) * P)
                for i, (a, b) in enumerate(((Q_hi, K_hi), (Q_hi, K_lo), (Q_lo, K_hi))):
                    mm = nc.tensor.matmul(out_ap, a[head][:, q], b[head][:, k0:k0 + w],
                                          start=(i == 0), stop=(i == 2 and not last_chunk))
                if last_chunk:
                    mm = nc.tensor.matmul(out_ap[:, w - P:w], identb[:], mask[:], start=False, stop=True)
                mm.then_inc(scores_ready, 1)

            def turn(ph, g):
                ps = slot(ph, ("T", g))
                pe_eng.wait_ge(exp_done, ph.pair * STEPS + g + 1)
                for b in range(chunk(g)[4] // P):
                    last = nc.tensor.transpose(ps[:, b * P:(b + 1) * P], prob[:, g % NP_RING, b * P:(b + 1) * P], ident[:])
                last.then_inc(slot_ready, 1)

            def weigh(ph, g):
                _, _, tile_no, k0, w, first, last_chunk = chunk(g)
                pe_eng.wait_ge(dve_freed, ph.after("dve", ("T", g)))
                if g % SBANKS == 0:
                    pe_eng.wait_ge(o_copied, 1 + ph.pair * NT + g // SBANKS)
                c0 = tile_no % 2 * VW
                n = w // P
                for b in range(n):
                    kb = k0 // P + b
                    c = slice(b * P, (b + 1) * P)
                    hi, lo = pT_hi[:, g % PT_RING, c], pT_lo[:, g % PT_RING, c]
                    nc.tensor.matmul(o_ps[:, c0:c0 + VW], hi, v[:, kb, 0:VW], start=(first and b == 0), stop=False)
                    last = nc.tensor.matmul(o_ps[:, c0:c0 + LORA + 1], lo, v[:, kb, 0:LORA + 1], start=False, stop=(last_chunk and b == n - 1))
                last.then_inc(pv_done, 1)

            def ffn_job(ph, name):
                ps = slot(ph, name)
                if name == FFN_UP[0]:
                    pe_eng.wait_ge(pool_done, ph.pool_after("down_scaled"))
                if name in FFN_UP:
                    w, k, half = name
                    for j in range(IT // 2):
                        last = nc.tensor.transpose(ps[:, j * P:(j + 1) * P], up_raw[:, w, half * (IT // 2) + j, k * P:(k + 1) * P], ident[:])
                else:
                    for j in range(2):
                        for k in range(KE):
                            c = (2 * name[1] + j) * P
                            last = nc.tensor.transpose(ps[:, j * E + k * P:j * E + (k + 1) * P], down_raw[:, k, c:c + P], ident[:])
                last.then_inc(slot_ready, 1)

            def job(ph, name):
                if name in FFN_UP + FFN_DOWN:
                    ffn_job(ph, name)
                elif name.startswith("out") or name == "wvo":
                    out_job(ph, name, ph.pair)
                else:
                    prep_job(ph, name, ph.pair + 2)

            def pair_program(ph, jobs, prep):
                for s in range(STEPS):
                    turn(ph, s)
                    if s + SBANKS < STEPS:
                        scores(s + SBANKS, ph.pool_after("qb_pe_lo"))
                    elif prep:
                        scores(s + SBANKS, ph.pool_after("qa_pe_lo"))
                    if s in jobs:
                        job(ph, jobs[s][0])
                    for g in weigh_at(s):
                        weigh(ph, g)
                for g in WEIGH_END:
                    weigh(ph, g)

            ph = setup_ph
            pe_eng.wait_ge(pool_done, ph.pool_after("ident"))
            for n in range(NG):
                pe_eng.wait_ge(xn_done, BLK * (n + 1))
                for k in range(KE):
                    ps = slot(ph, ("xT", n, k))
                    for j in range(BLK):
                        last = nc.tensor.transpose(ps[:, j * P:(j + 1) * P], acc[:, BLK * n + j, k * P:(k + 1) * P], ident[:])
                    last.then_inc(slot_ready, 1)
            pe_eng.wait_ge(wkva_done, 2)
            for n in range(NG):
                ps = slot(ph, ("kv", n))
                pe_eng.wait_ge(dve_freed, ph.after("dve", ("xT", n, KE - 1)))
                for j in range(BLK):
                    last = exact(ps[:, j * P:(j + 1) * P], [(*a, wkva_hi[:, k, :], wkva_lo[:, k, :]) for k, a in enumerate(x_tile(BLK * n + j))])
                last.then_inc(slot_ready, 1)
            for n in range(NG):
                for side in "BA":
                    ps = slot(ph, ("K", n, side))
                    if side == "B":
                        pe_eng.wait_ge(kcat_done, n + 1)
                        pe_eng.wait_ge(pool_done, ph.pool_after(f"kr{n}.5"))
                    c = 0 if side == "B" else LORA
                    for j in range(BLK):
                        last = nc.tensor.transpose(ps[:, j * P:(j + 1) * P], kcat[:, BLK * n + j, c:c + P], ident[:])
                    last.then_inc(slot_ready, 1)
            for name, _ in PREP_FIRST:
                prep_job(ph, name, 1)
            if "pad" in SETUP.at:
                ps = slot(ph, "pad")
                nc.tensor.transpose(ps[:, 0:P], ident[:], ident[:]).then_inc(slot_ready, 1)
            for g in range(SBANKS):
                scores(g, ph.pool_after("qa_pe_lo"))
            with pe_eng.Fori(0, PAIRS - 1) as p:
                pair_program(loop_ph.of_pair(p), LOOP_JOBS, True)
            pair_program(last_ph, LAST_JOBS, False)
            ph = tail_ph

            def gate_up(n):
                for it in range(IT):
                    j = n * IT + it
                    if j >= 2:
                        pe_eng.wait_ge(hid_done, j - 1)
                    if j == 0:
                        pe_eng.wait_ge(dve_freed, last_ph.after("dve", FFN_DOWN[-1]))
                    c = slice(n * BANK, (n + 1) * BANK)
                    i = slice(it * P, (it + 1) * P)
                    for w in range(2):
                        last = exact(s_ps[:, 2 * (j % 2) + w, :], [
                            (upT_hi[:, w, k, i], upT_lo[:, w, k, i], xT_hi[:, k, c], xT_lo[:, k, c]) for k in range(KE)])
                    last.then_inc(gu_ready, 1)
                    if j < len(OUT_LAST):
                        out_job(tail_ph, OUT_LAST[j][0], PAIRS)

            def down(n):
                pe_eng.wait_ge(hid_lo_done, IT * (n + 1))
                for tp in range(2):
                    u = 2 * n + tp
                    if u >= 2:
                        pe_eng.wait_ge(gate_done, u - 1)
                    for j in range(2):
                        c = slice((2 * tp + j) * P, (2 * tp + j + 1) * P)
                        bank = s_ps[:, SBANKS - 1, :] if u % 2 else o_ps[:, :]
                        last = exact(bank[:, j * E:(j + 1) * E], [
                            (hid_hi[:, n % 2, it, c], hid_lo[:, n % 2, it, c], downT_hi[:, it, :], downT_lo[:, it, :]) for it in range(IT)])
                    last.then_inc(down_ready, 1)

            gate_up(0)
            for n in range(1, NG):
                gate_up(n)
                down(n - 1)
            down(NG - 1)

        @block.scalar
        def _(act):
            def copy(dst, src):
                return nc.scalar.activation(dst, src, ACT.Copy)

            def slot_of(ph, name):
                act.wait_ge(slot_ready, ph.after("ready", name))
                return slot_ps[:, ph.slots.at[name] % 2, :]

            def prep_job(ph, name):
                ps = slot_of(ph, name)
                if name == "wqT":
                    copy(wqT[:].rearrange("p h k e -> p (h k e)"), ps).then_inc(act_freed, 1)
                elif name == "wkvT":
                    blocks = ps.rearrange("p (h v c) -> p h v c", h=2, v=2)
                    copy(wkT[:], blocks[:, :, 0, 0:LORA])
                    copy(wvT[:, 0, 0:LORA], blocks[:, 0, 1, 0:LORA])
                    copy(wvT[:, 1, LORA:P], blocks[:, 1, 1, 0:LORA]).then_inc(act_freed, 1)
                elif name == "wabs":
                    copy(wabs_hi[:].rearrange("p k c -> p (k c)"), ps[:, 0:KE * P]).then_inc(hi_done, 1)
                elif name.startswith("lat"):
                    n = int(name[3:])
                    if ph is not setup_ph:
                        act.wait_ge(pool_done, ph.pool_after("qb_pe_lo"))
                    copy(lat[:, n * BANK:(n + 1) * BANK], ps).then_inc(act_freed, 1)
                elif name.startswith("peT"):
                    n = int(name[3:])
                    if ph is not setup_ph:
                        act.wait_ge(pool_done, ph.pool_after("qb_pe_lo"))
                    copy(pe[:, n * BANK:(n + 1) * BANK], ps).then_inc(act_freed, 1)
                elif name == "pad":
                    copy(spare[:, 0:1], ps[:, 0:1]).then_inc(act_freed, 1)
                else:
                    n = int(name[2:])
                    if n >= 2:
                        act.wait_ge(pool_done, ph.pool_after(f"rope{n - 2}.4"))
                    copy(qtok[:, n % 2].rearrange("p t c -> p (t c)"), ps).then_inc(act_freed, 1)

            def out_job(ph, name):
                if name == "wvo":
                    copy(wvo_hi[:], slot_of(ph, name)[:, 0:E]).then_inc(hi_done, 1)
                elif name.startswith("outT"):
                    copy(oT_hi[:, int(name[4]) % 2, :], slot_of(ph, name)).then_inc(hi_done, 1)

            def exponentials(pair, g):
                _, _, tile_no, _, w, first, _ = chunk(g)
                if first:
                    act.wait_ge(max_ready, (pair + g // STEPS) * 2 * NT + tile_no + 1)
                nc.scalar.activation(prob[:, g % NP_RING, 0:w], s_ps[:, g % SBANKS, 0:w], ACT.Exp,
                                     bias=neg_max[:, tile_no % TILE_RING:tile_no % TILE_RING + 1]).then_inc(exp_done, 1)

            def copy_outputs(ph, r):
                act.wait_ge(pv_done, ph.pair * STEPS + SBANKS * (r + 1))
                copy(o_raw[:, r % 2].rearrange("p t c -> p (t c)"), o_ps[:, 0:2 * VW]).then_inc(o_copied, 1)

            def turned_hi(ph, g):
                w = chunk(g)[4]
                copy(pT_hi[:, g % PT_RING, 0:w], slot_of(ph, ("T", g))[:, 0:w]).then_inc(hi_done, 1)

            def ffn_job(ph, name):
                ps = slot_of(ph, name)
                if name == FFN_UP[0]:
                    act.wait_ge(scores_ready, ph.pair * STEPS + NCH)
                if name in FFN_UP:
                    w, k, half = name
                    c = IT // 2 * P
                    copy(upT_hi[:, w, k, half * c:(half + 1) * c], ps[:, 0:c]).then_inc(hi_done, 1)
                else:
                    i = name[1]
                    copy(downT_hi[:, 2 * i:2 * i + 2, :].rearrange("p t e -> p (t e)"), ps).then_inc(hi_done, 1)

            def job(ph, name):
                if name in FFN_UP + FFN_DOWN:
                    ffn_job(ph, name)
                elif name.startswith("out") or name == "wvo":
                    out_job(ph, name)
                else:
                    prep_job(ph, name)

            def pair_program(ph, jobs, prep):
                for s in range(STEPS):
                    if s + 1 < STEPS or prep:
                        exponentials(ph.pair, s + 1)
                    if s % SBANKS == 3 and s > SBANKS:
                        copy_outputs(ph, s // SBANKS - 1)
                    turned_hi(ph, s)
                    if s in jobs:
                        job(ph, jobs[s][0])
                copy_outputs(ph, STEPS // SBANKS - 1)

            ph = setup_ph
            for n in range(NG):
                for k in range(KE):
                    copy(xT_hi[:, k, n * BANK:(n + 1) * BANK], slot_of(ph, ("xT", n, k))).then_inc(hi_done, 1)
            for n in range(NG):
                copy(kraw[:, BLK * n:BLK * n + BLK, :].rearrange("p t c -> p (t c)"), slot_of(ph, ("kv", n))).then_inc(act_freed, 1)
            for n in range(NG):
                for side in "BA":
                    copy(K_hi["AB".index(side)][:, n * BANK:(n + 1) * BANK], slot_of(ph, ("K", n, side))).then_inc(hi_done, 1)
            for name, _ in PREP_FIRST:
                if name == "wabs":
                    pass
                prep_job(ph, name)
            if "pad" in SETUP.at:
                prep_job(ph, "pad")
            copy(spare[:, 1:2], ones[:]).then_inc(o_copied, 1)
            exponentials(0, 0)
            with act.Fori(0, PAIRS - 1) as p:
                pair_program(loop_ph.of_pair(p), LOOP_JOBS, True)
            pair_program(last_ph, LAST_JOBS, False)
            def hidden_hi(j):
                n, it = divmod(j, IT)
                act.wait_ge(hid_done, j + 1)
                if n >= 2:
                    act.wait_ge(down_ready, 2 * (n - 1))
                copy(hid_hi[:, n % 2, it, :], hid[:, j % 2, :]).then_inc(hid_hi_done, 1)

            def out_gate(u):
                act.wait_ge(down_ready, u + 1)
                if u >= 2:
                    act.wait_ge(gated, u - 1)
                bank = s_ps[:, SBANKS - 1, :] if u % 2 else o_ps[:, :]
                nc.scalar.activation(gate[:, u % 2].rearrange("p t e -> p (t e)"), bank, ACT.Silu).then_inc(gate_done, 1)

            for j in range(NG * IT):
                act.wait_ge(gu_ready, j + 1)
                if j >= 2:
                    act.wait_ge(hid_done, j - 1)
                nc.scalar.activation(silu_g[:, j % 2, :], s_ps[:, 2 * (j % 2), :], ACT.Silu).then_inc(silu_done, 1)
                if j < len(OUT_LAST):
                    out_job(tail_ph, OUT_LAST[j][0])
                if j >= 1:
                    hidden_hi(j - 1)
                if j % IT == 3 and j >= 2 * IT:
                    out_gate(2 * (j // IT) - 4)
                    out_gate(2 * (j // IT) - 3)
            hidden_hi(NG * IT - 1)
            for u in range(2 * NG - 4, 2 * NG):
                out_gate(u)

        @block.vector
        def _(dve):
            steps = [0]

            def then_wait(instruction):
                steps[0] += 1
                instruction.then_inc(dve_setup, 1)
                dve.wait_ge(dve_setup, steps[0])

            def lo_of(ph, name, dst, hi, cols=slice(0, BANK)):
                dve.wait_ge(hi_done, ph.after("hi", name))
                ps = slot_ps[:, ph.slots.at[name] % 2, cols]
                nc.vector.tensor_tensor(dst, ps, hi, ALU.subtract).then_inc(dve_freed, 1)

            def f32(ap):
                return ap.bitcast(F32)

            def out_job(ph, name):
                if name == "wvo":
                    lo_of(ph, name, wvo_lo[:], f32(wvo_hi[:]), slice(0, E))
                    return
                q = int(name[4])
                if name.startswith("outT"):
                    lo_of(ph, name, oT_lo[:, q % 2, :], f32(oT_hi[:, q % 2, :]))
                    return
                half = "ab".index(name[5])
                high, low = TILE_ORDER[4 * q + 2 * half:4 * q + 2 * half + 2]
                tiles = acc[:, low:high + 1:high - low, :]
                dve.wait_ge(slot_ready, ph.after("ready", name))
                ps = slot_ps[:, ph.slots.at[name] % 2, :].rearrange("p (t e) -> p t e", t=2)
                nc.vector.tensor_tensor(tiles, ps, tiles, ALU.add).then_inc(dve_freed, 1)

            def row_max(pair, g):
                _, _, tile_no, k0, w, first, last_chunk = chunk(g)
                pair = pair + g // STEPS
                g %= STEPS
                r = tile_no % TILE_RING
                c = k0 // BANK
                dve.wait_ge(scores_ready, pair * STEPS + g + 1)
                src = s_ps[:, g % SBANKS, 0:w]
                if first and last_chunk:
                    nc.vector.tensor_reduce(neg_max[:, r:r + 1], src, AX.X, ALU.max, negate=True).then_inc(max_ready, 1)
                    return
                nc.vector.tensor_reduce(part_max[:, r, c:c + 1], src, AX.X, ALU.max).then_inc(part_done, 1)
                if last_chunk:
                    dve.wait_ge(part_done, pair * PARTS + part_of[g])
                    nc.vector.tensor_reduce(neg_max[:, r:r + 1], part_max[:, r, 0:c + 1], AX.X, ALU.max, negate=True).then_inc(max_ready, 1)

            def normalise(ph, r):
                head, high = chunk(SBANKS * r)[:2]
                low = NT - 1 - high
                b = r % 2
                done = ph.pair * NT + r + 1
                dve.wait_ge(o_copied, 1 + done)
                nc.vector.tensor_tensor(o_sum[:, b], o_raw[:, b, :, 0:LORA], o_raw[:, b, :, LORA + 1:VW], ALU.add)
                nc.vector.reciprocal(rinv[:, b, :], o_raw[:, b, :, LORA]).then_inc(summed, 1)
                dve.wait_ge(summed, done)
                nc.vector.tensor_tensor(o_pair[:, high:(low - 1 if low else None):low - high, head * LORA:(head + 1) * LORA], o_sum[:, b],
                                        rinv[:, b, :].unsqueeze(2).to_broadcast([P, 2, LORA]), ALU.mult).then_inc(norm_done, 1)

            def ffn_job(ph, name):
                if name in FFN_UP:
                    w, k, half = name
                    c = slice(half * (IT // 2 * P), (half + 1) * (IT // 2 * P))
                    lo_of(ph, name, upT_lo[:, w, k, c], f32(upT_hi[:, w, k, c]), slice(0, IT // 2 * P))
                else:
                    tiles = slice(2 * name[1], 2 * name[1] + 2)
                    lo_of(ph, name, downT_lo[:, tiles, :].rearrange("p t e -> p (t e)"), f32(downT_hi[:, tiles, :].rearrange("p t e -> p (t e)")))

            def job(ph, name):
                if name in FFN_UP + FFN_DOWN:
                    ffn_job(ph, name)
                elif name.startswith("out") or name == "wvo":
                    out_job(ph, name)
                elif name == "wabs":
                    lo_of(ph, name, wabs_lo[:].rearrange("p k c -> p (k c)"), f32(wabs_hi[:].rearrange("p k c -> p (k c)")), slice(0, KE * P))

            def pair_program(ph, jobs, prep):
                for s in range(STEPS):
                    w = chunk(s)[4]
                    lo_of(ph, ("T", s), pT_lo[:, s % PT_RING, 0:w], pT_hi[:, s % PT_RING, 0:w], slice(0, w))
                    if s + SBANKS < STEPS or prep:
                        row_max(ph.pair, s + SBANKS)
                    if s in jobs:
                        job(ph, jobs[s][0])
                    if s % SBANKS == 3 and s > SBANKS:
                        normalise(ph, s // SBANKS - 1)
                normalise(ph, STEPS // SBANKS - 1)

            def stats(n):
                dve.wait_ge(x_loaded[n], 16)
                for t in range(BLK * n, BLK * n + BLK):
                    last = nc.vector.bn_stats(stat[:, t, :], acc[:, t, :])
                then_wait(last)
                for t in range(BLK * n, BLK * n + BLK):
                    last = nc.vector.bn_aggr(mv[:, t, :], stat[:, t, :])
                then_wait(last)
                then_wait(nc.vector.tensor_scalar(var_eps[:, BLK * n:BLK * n + BLK], mv[:, BLK * n:BLK * n + BLK, 1], EPS_LN, None, ALU.add))

            ph = setup_ph
            stats(0)
            nc.vector.memset(wvT[:], 0.0)
            then_wait(nc.vector.memset(wkvs[:], 0.0))
            nc.vector.memset(v[:], 1.0)
            for n in range(NG):
                if n + 1 < NG:
                    stats(n + 1)
                dve.wait_ge(pool_done, ph.pool_after(f"rstd{n}"))
                for t in range(BLK * n, BLK * n + BLK):
                    nc.vector.tensor_scalar(acc[:, t, :], acc[:, t, :], mv[:, t, 0:1], rstd[:, t:t + 1],
                                            ALU.subtract, ALU.mult).then_inc(xn_done, 1)
            dve.wait_ge(consts_loaded, 64)
            nc.vector.tensor_copy(wkva_hi[:], wkva_sb[:]).then_inc(wkva_done, 1)
            dve.wait_ge(wkva_done, 1)
            nc.vector.tensor_tensor(wkva_lo[:], wkva_sb[:], f32(wkva_hi[:]), ALU.subtract).then_inc(wkva_done, 1)
            for n in range(NG):
                for k in range(KE):
                    c = slice(n * BANK, (n + 1) * BANK)
                    lo_of(ph, ("xT", n, k), xT_lo[:, k, c], f32(xT_hi[:, k, c]))

            def squares(n):
                tiles = slice(BLK * n, BLK * n + BLK)
                ckv = kraw[:, tiles, 0:LORA]
                dve.wait_ge(act_freed, ph.after("act", ("kv", n)))
                then_wait(nc.vector.tensor_tensor(sq[:], ckv, ckv, ALU.mult))
                then_wait(nc.vector.tensor_reduce(ss[:, tiles], sq[:], AX.X, ALU.add))
                then_wait(nc.vector.tensor_scalar(ms_eps[:, tiles], ss[:, tiles], 1.0 / LORA, EPS_RMS, ALU.mult, ALU.add))

            def values_and_keys(n):
                tiles = slice(BLK * n, BLK * n + BLK)
                dve.wait_ge(pool_done, ph.pool_after(f"rms{n}"))
                then_wait(nc.vector.tensor_tensor(kn[:, tiles, :], kraw[:, tiles, 0:LORA],
                                                  rms[:, tiles].unsqueeze(2).to_broadcast([P, BLK, LORA]), ALU.mult))
                then_wait(nc.vector.tensor_copy(v[:, tiles, 0:LORA], kn[:, tiles, :]))
                nc.vector.tensor_tensor(v[:, tiles, LORA + 1:VW], kn[:, tiles, :], v[:, tiles, 0:LORA], ALU.subtract)
                nc.vector.tensor_scalar(kcat[:, tiles, 0:LORA], kn[:, tiles, :], SCALE, None, ALU.mult)
                nc.vector.tensor_scalar(kcat[:, tiles, 2 * LORA:3 * LORA], kn[:, tiles, :], SCALE, None, ALU.mult).then_inc(kcat_done, 1)

            squares(0)
            for n in range(NG):
                if n + 1 < NG:
                    squares(n + 1)
                values_and_keys(n)
            for n in range(NG):
                for side in "BA":
                    c = slice(n * BANK, (n + 1) * BANK)
                    i = "AB".index(side)
                    lo_of(ph, ("K", n, side), K_lo[i][:, c], f32(K_hi[i][:, c]))
            nc.vector.memset(acc[:], 0.0)
            nc.vector.memset(f32(wvo_hi[:]), 0.0)
            nc.vector.memset(f32(wvo_lo[:]), 0.0)
            nc.vector.memset(o_pair[:], 0.0).then_inc(norm_done, 1)
            lo_of(ph, "wabs", wabs_lo[:].rearrange("p k c -> p (k c)"), f32(wabs_hi[:].rearrange("p k c -> p (k c)")), slice(0, KE * P))
            for g in range(SBANKS):
                row_max(0, g)
            with dve.Fori(0, PAIRS - 1) as p:
                pair_program(loop_ph.of_pair(p), LOOP_JOBS, True)
            pair_program(last_ph, LAST_JOBS, False)
            def finish(u):
                tiles = slice(2 * u, 2 * u + 2)
                dve.wait_ge(gate_done, u + 1)
                if u >= 2:
                    dve.wait_ge(stored[u % 2], 16 * (u // 2))
                nc.vector.tensor_tensor(y[:, u % 2], gate[:, u % 2], acc[:, tiles, :], ALU.mult).then_inc(gated, 1)
                dve.wait_ge(gated, u + 1)
                if u == 0:
                    dve.wait_ge(x_again, 16)
                nc.vector.tensor_tensor(y[:, u % 2], y[:, u % 2], x_in[:, tiles, :], ALU.add).then_inc(y_done, 1)

            for j in range(NG * IT):
                dve.wait_ge(silu_done, j + 1)
                if j >= 2:
                    dve.wait_ge(hid_lo_done, j - 1)
                nc.vector.tensor_tensor(hid[:, j % 2, :], s_ps[:, 2 * (j % 2) + 1, :], silu_g[:, j % 2, :], ALU.mult).then_inc(hid_done, 1)
                if j < len(OUT_LAST):
                    out_job(tail_ph, OUT_LAST[j][0])
                if j % IT == 4 and j >= 2 * IT:
                    finish(2 * (j // IT) - 4)
                    finish(2 * (j // IT) - 3)
            for u in range(2 * NG - 4, 2 * NG):
                finish(u)

        @block.gpsimd
        def _(pool):
            def run(ph, name, issue, *waits):
                value = ph.pool_after(name)
                if ph is not setup_ph or ph.pool.after[name] > 1:
                    pool.wait_ge(pool_done, value - 1)
                for s, v in waits:
                    pool.wait_ge(s, v)
                issue().then_inc(pool_done, 1)

            def tt(dst, a, b, op):
                return lambda: nc.gpsimd.tensor_tensor(dst, a, b, op)

            def split_queries(ph, head, *waits):
                h = "qa" if head == 0 else "qb"
                lat_rows = slice(LORA, P) if head == 0 else slice(0, LORA)
                pe_rows = slice(0, LORA) if head == 0 else slice(LORA, P)
                for what, src, rows in (("lat", lat, lat_rows), ("pe", pe, pe_rows)):
                    run(ph, f"{h}_{what}_hi", tt(Q_hi[head][rows, :], src[rows, :], ones[rows, :].to_broadcast([LORA, S]), ALU.mult), *waits)
                    run(ph, f"{h}_{what}_lo", tt(Q_lo[head][rows, :], src[rows, :], Q_hi[head][rows, :].bitcast(F32), ALU.subtract))
                    waits = ()

            def weights(ph, pairs):
                free = () if ph is setup_ph else ((slot_ready, ph.base["ready"]),)
                pew = wq_sb[:].rearrange("p k (h c) -> p k h c", h=2)[:, :, :, NOPE:NOPE + ROPE]
                run(ph, "wpe_hi", tt(wpe_hi[:], pew, ones[:].unsqueeze(2).unsqueeze(3).to_broadcast([P, KE, 2, ROPE]), ALU.mult), (wq_loaded, 16 * pairs), *free)
                run(ph, "wpe_lo", tt(wpe_lo[:], pew, wpe_hi[:].bitcast(F32), ALU.subtract))
                run(ph, "wkvs", tt(wkvs[0:LORA, :], wkv_sb[:], scale_sb[:].to_broadcast([LORA, KVW]), ALU.mult),
                    (wkv_loaded, 16 * pairs), (consts_loaded, 64), (dve_setup, 4))

            def rotate(ph, step, src, dst, c_buf, s_buf, n, parts, *waits):
                half = ROPE // 2
                tiles = slice(BLK * n, BLK * n + BLK)

                def table(tab, m):
                    return tab[:, tiles, :].unsqueeze(2).to_broadcast([P, BLK, m, half])

                def halves(ap, i):
                    return ap.rearrange("p t (m x d) -> p t m x d", m=parts, x=2)[:, :, :, i, :]

                whole = lambda ap: ap.rearrange("p t (m d) -> p t m d", d=half)
                run(ph, step(0), tt(whole(c_buf), whole(src), table(cos_sb, 2 * parts), ALU.mult), *waits)
                run(ph, step(1), tt(halves(s_buf, 0), halves(src, 1), table(sin_sb, parts), ALU.mult))
                run(ph, step(2), tt(halves(s_buf, 1), halves(src, 0), table(sin_sb, parts), ALU.mult))
                run(ph, step(3), tt(halves(dst, 0), halves(c_buf, 0), halves(s_buf, 0), ALU.subtract))
                run(ph, step(4), tt(halves(dst, 1), halves(c_buf, 1), halves(s_buf, 1), ALU.add))

            def rotate_queries(ph):
                for n in range(NG):
                    waits = [(act_freed, ph.after("act", f"pe{n}"))]
                    if n >= 2:
                        waits.append((slot_ready, ph.after("ready", f"peT{n - 2}")))
                    rotate(ph, lambda i: f"rope{n}.{i}", qtok[:, n % 2], qrot[:, n % 2], rope_c[:], rope_s[:], n, 2, *waits)

            ph = setup_ph
            run(ph, "half", lambda: nc.gpsimd.memset(minus_half[:], -0.5))
            run(ph, "ones", lambda: nc.gpsimd.memset(ones[:], 1.0))
            run(ph, "ident0", lambda: nc.gpsimd.memset(ident[:], 0.0))
            run(ph, "ident", lambda: nc.gpsimd.affine_select(out=ident[:], in_=ident[:], compare_op=ALU.not_equal, fill=1.0,
                                                             base=0, pattern=[[-1, P]], channel_multiplier=1))
            for n in range(NG):
                c = slice(BLK * n, BLK * n + BLK)
                run(ph, f"rstd{n}", tt(rstd[:, c], var_eps[:, c], minus_half[:], ALU.pow), (dve_setup, 3 * (n + 1) + (n > 0)))
            run(ph, "identb", lambda: nc.gpsimd.tensor_copy(identb[:], ident[:]))
            run(ph, "mask0", lambda: nc.gpsimd.memset(mask[:], 0.0))
            run(ph, "mask", lambda: nc.gpsimd.affine_select(out=mask[:], in_=mask[:], compare_op=ALU.is_ge, fill=MASKED,
                                                            base=0, pattern=[[-1, P]], channel_multiplier=1))
            for n in range(NG):
                c = slice(BLK * n, BLK * n + BLK)
                step = 3 * NG + 1 + 3 * (n + 1) + 2 * max(n - 1, 0)
                run(ph, f"rms{n}", tt(rms[:, c], ms_eps[:, c], minus_half[:], ALU.pow), (dve_setup, step))
                rotate(ph, lambda i: f"kr{n}.{i}", kraw[:, c, LORA:P], krot[:, c, :], krope_c[:, c, :], krope_s[:, c, :], n, 1,
                       (act_freed, ph.after("act", ("kv", n))), (consts_loaded, 64))
                run(ph, f"kr{n}.5", lambda: nc.gpsimd.tensor_scalar(kcat[:, c, LORA:2 * LORA], krot[:, c, :], SCALE, 1.0, ALU.mult, ALU.mult))
            weights(ph, 1)
            rotate_queries(ph)
            split_queries(ph, 0, (act_freed, ph.after("act", "lat3")), (act_freed, ph.after("act", "peT3")))
            with pool.Fori(0, PAIRS - 1) as p:
                ph = loop_ph.of_pair(p)
                split_queries(ph, 1, (scores_ready, p * STEPS + SBANKS), (act_freed, ph.base["act"]))
                weights(ph, p + 2)
                rotate_queries(ph)
                split_queries(ph, 0, (act_freed, ph.after("act", "lat3")), (act_freed, ph.after("act", "peT3")),
                              (scores_ready, p * STEPS + NCH))
            split_queries(last_ph, 1, (scores_ready, (PAIRS - 1) * STEPS + SBANKS), (act_freed, last_ph.base["act"]))
            ph = last_ph
            run(ph, "up_zero", lambda: nc.gpsimd.memset(up_raw[:, :, IT - 1, :], 0.0))
            run(ph, "up_scale_zero", lambda: nc.gpsimd.memset(up_scale[:], 0.0))
            run(ph, "down_zero", lambda: nc.gpsimd.memset(down_raw[:, :, INTER:IT * P], 0.0))
            for w in range(2):
                run(ph, f"up_scaled{w}", tt(up_raw[:, w], up_raw[:, w], up_scale[:, w, :].unsqueeze(2).to_broadcast([P, IT, E]), ALU.mult), (ffn_loaded, 16 * 10))
            run(ph, "down_scaled", tt(down_raw[:], down_raw[:], down_scale[:].unsqueeze(2).to_broadcast([P, KE, IT * P]), ALU.mult))

            for j in range(NG * IT):
                n, it = divmod(j, IT)
                pool.wait_ge(hid_hi_done, j + 1)
                nc.gpsimd.tensor_tensor(hid_lo[:, n % 2, it, :], hid[:, j % 2, :], hid_hi[:, n % 2, it, :].bitcast(F32), ALU.subtract).then_inc(hid_lo_done, 1)


_INS = ["L0_attn_x", "L0_attn_wq", "L0_attn_wkv_a", "L0_attn_wkv_b", "L0_attn_wo", "L0_attn_kv_norm_scale",
        "L0_ffn_gate_w", "L0_ffn_up_w", "L0_ffn_down_w", "L0_ffn_gate_s", "L0_ffn_up_s", "L0_ffn_down_s"]


def kernel(**inputs):
    import numpy as _np
    import concourse.bacc as _bacc
    from concourse import mybir as _mybir
    from concourse.bass_utils import run_bass_kernel_spmd as _run

    nc = _bacc.Bacc("TRN2", target_bir_lowering=False, num_devices=1)
    inv = (1.0 / _np.float32(10000.0) ** (_np.arange(0, ROPE, 2, dtype=_np.float32) / _np.float32(ROPE))).astype(_np.float32)
    angle = _np.arange(S, dtype=_np.float32)[:, None] * inv
    arrays = {"cos_dram": _np.cos(angle.astype(_np.float64)).astype(_np.float32),
              "sin_dram": _np.sin(angle.astype(_np.float64)).astype(_np.float32)}
    args = []
    for name in _INS:
        a = _np.ascontiguousarray(inputs[name])
        arrays[f"in_{name}_dram"] = a
        args.append(nc.dram_tensor(f"in_{name}_dram", a.shape, _mybir.dt.from_np(a.dtype), kind="ExternalInput").ap())
    for name in ("cos_dram", "sin_dram"):
        args.append(nc.dram_tensor(name, (S, ROPE // 2), F32, kind="ExternalInput").ap())
    args.append(nc.dram_tensor("out_0_dram", (1, S, E), F32, kind="ExternalOutput").ap())
    mla_gated_ffn_kernel(nc, *args)
    r = _run(nc, [arrays], core_ids=[0])
    return r.results[0]["out_0_dram"]
```

```python
from contextlib import ExitStack

import concourse.bass as bass
import concourse.mybir as mybir

F32 = mybir.dt.float32
F32R = mybir.dt.float32r
F16 = mybir.dt.float16
BF16 = mybir.dt.bfloat16
ALU = mybir.AluOpType
ACT = mybir.ActivationFunctionType
AX = mybir.AxisListType

P = 128
S, E = 2048, 256
H, NOPE, ROPE, VD, LORA = 16, 128, 64, 128, 64
INTER = 704
EPS_LN, EPS_RMS = 1e-5, 1e-6
SCALE = float((NOPE + ROPE) ** -0.5)
MASKED = -3.0e38
NT = S // P
KE = E // P
BANK = 512
BLK = BANK // P
NG = NT // BLK
PAIRS = H // 2
QW = 2 * (NOPE + ROPE)
KVW = 2 * (NOPE + VD)
IT = -(-INTER // P)
SBANKS = 5
NP_RING, PT_RING, TILE_RING = 3, 5, 4
VW = 2 * LORA + 1

TILE_ORDER = [t for k in range(NT // 2) for t in (NT - 1 - k, k)]
CHUNKS = []
for pos, t in enumerate(TILE_ORDER):
    keys = (t + 1) * P
    for k0 in range(0, keys, BANK):
        CHUNKS.append((t, pos, k0, min(BANK, keys - k0), k0 == 0, k0 + BANK >= keys))
NCH = len(CHUNKS)
STEPS = 2 * NCH


WEIGH = {0: (-3,), 1: (-3,), 2: (-3,), 3: (), 4: (-4, -3)}


def weigh_at(step):
    return [step + d for d in WEIGH[step % SBANKS] if step + d >= 0]


WEIGH_END = range(STEPS - 3, STEPS)


def chunk(g):
    g %= STEPS
    t, pos, k0, w, first, last = CHUNKS[g % NCH]
    head = g // NCH
    return head, t, head * NT + pos, k0, w, first, last


class Slots:

    def __init__(self):
        self.kinds, self.counts, self.at = [], [], {}
        self.count = {"ready": 0, "hi": 0, "act": 0, "dve": 0}

    def add(self, name, kind):
        self.count["ready"] += 1
        if kind == "split":
            self.count["hi"] += 1
        self.count["act" if kind == "act" else "dve"] += 1
        self.kinds.append(kind)
        self.counts.append(dict(self.count))
        self.at[name] = len(self.kinds) - 1


class Phase:

    def __init__(self, slots, pool, base, pool_base, pair=None):
        self.slots, self.pool, self.base, self.pool_base, self.pair = slots, pool, base, pool_base, pair

    def of_pair(self, pair):
        base = {k: self.base[k] + pair * self.slots.count[k] for k in self.base}
        return Phase(self.slots, self.pool, base, self.pool_base + pair * len(self.pool.names), pair)

    def after(self, kind, name):
        return self.base[kind] + self.slots.counts[self.slots.at[name]][kind]

    def pool_after(self, name):
        return self.pool_base + self.pool.after[name]

    def end(self, times=1):
        return {k: self.base[k] + times * self.slots.count[k] for k in self.base}


SPLIT, BY_ACT, BY_DVE = "split", "act", "dve"

QUERY_ORDER = (0, 3, 1, 2)


def query_cols(i):
    return slice(QUERY_ORDER[i] * BANK, (QUERY_ORDER[i] + 1) * BANK)


OUT_JOBS = {
    4: ("outT3", SPLIT), 7: ("outP3a", BY_DVE), 9: ("outP3b", BY_DVE), 13: ("wvo", SPLIT), 59: ("outT0", SPLIT),
    63: ("outP0a", BY_DVE), 65: ("outP0b", BY_DVE), 69: ("outT1", SPLIT), 71: ("outP1a", BY_DVE), 74: ("outP1b", BY_DVE),
    75: ("outT2", SPLIT), 76: ("outP2a", BY_DVE), 79: ("outP2b", BY_DVE)}
PREP_JOBS = {
    11: ("wqT", BY_ACT), 12: ("pe0", BY_ACT), 14: ("wkvT", BY_ACT), 19: ("wabs", SPLIT), 28: ("pe1", BY_ACT),
    30: ("lat0", BY_ACT), 39: ("lat1", BY_ACT), 42: ("pe2", BY_ACT), 44: ("lat2", BY_ACT), 47: ("pe3", BY_ACT),
    49: ("lat3", BY_ACT)}
FFN_UP = [(w, k, half) for w in range(2) for k in range(KE) for half in range(2)]
FFN_DOWN = [(2, i) for i in range(IT // 2)]
FFN_JOBS = {s: (name, SPLIT) for s, name in zip((37, 39, 41, 43, 45, 47, 49, 51, 54, 56, 61), FFN_UP + FFN_DOWN)}
QUERY_JOBS = [f"pe{n}" for n in range(NG)]
LOOP_JOBS, LAST_JOBS = {**OUT_JOBS, **PREP_JOBS}, {**OUT_JOBS, **FFN_JOBS}
OUT_LAST = [OUT_JOBS[s] for s in (4, 7, 9)]
PE_STEP = (
    ("turn", "job", "scores", "weigh"),
    ("turn", "scores", "job", "weigh"),
    ("turn", "weigh", "job", "scores"),
    ("turn", "scores", "weigh", "job"),
    ("turn", "weigh", "job", "scores"))
ACT_STEP = (
    ("exp", "hi", "job"),
    ("exp", "hi", "job"),
    ("exp", "hi", "outputs", "job"),
    ("exp", "hi", "job"),
    ("hi", "exp", "job"))
DVE_STEP = (
    ("lo", "job", "max"),
    ("lo", "job", "max"),
    ("lo", "job", "max"),
    ("lo", "max", "job"),
    ("lo", "normalise", "job", "max"))

SETUP_ORDER = [("xT", 0, 0), ("xT", 0, 1), ("xT", 1, 0), ("xT", 1, 1), ("kv", 0), "wqT", ("xT", 2, 0), ("xT", 2, 1), ("kv", 1),
               "wkvT", "pe0", ("xT", 3, 0), ("xT", 3, 1), ("kv", 2), "wabs", ("kv", 3), ("K", 0, "B"), ("K", 0, "A"),
               "lat0", "pe1", ("K", 1, "B"), ("K", 1, "A"), "lat1", ("K", 2, "B"), ("K", 2, "A"), "pe2",
               "lat2", "lat3", ("K", 3, "B"), ("K", 3, "A"), "pe3"]
WARM_UP = 44
SETUP_BANKS = 6


def pair_slots(jobs):
    slots = Slots()
    for s in range(STEPS):
        slots.add(("T", s), SPLIT)
        if s in jobs:
            slots.add(*jobs[s])
    return slots


SETUP = Slots()
for name in SETUP_ORDER:
    SETUP.add(name, SPLIT if name[0] in ("xT", "K") or name == "wabs" else BY_ACT)
LOOP, LAST = pair_slots(LOOP_JOBS), pair_slots(LAST_JOBS)
assert len(LOOP.kinds) % 2 == 0
TAIL = Slots()
for name, kind in OUT_LAST:
    TAIL.add(name, kind)

POOL_W = ["wpe_hi", "wpe_lo", "wkvs"]
POOL_KEY = [[f"rms{n}"] + [f"kr{n}.{i}" for i in range(6)] for n in range(NG)]
POOL_ROPES = [[f"rope{n}.{i}" for i in range(3)] for n in range(NG)]
POOL_SETUP = ["half", "ones", "ident0", "ident", "wkvs0", "wvT0", "v1", "identb", "mask0", "mask"] + [
    f"rstd{n}" for n in range(NG)] + POOL_W + POOL_KEY[0] + POOL_KEY[1] + POOL_ROPES[0] + POOL_KEY[2] + POOL_ROPES[1] + POOL_KEY[3] + POOL_ROPES[2] + POOL_ROPES[3]
POOL_QB = ["qb_lat_hi", "qb_lat_lo", "qb_pe_hi", "qb_pe_lo"]
POOL_ROPE = [step for steps in POOL_ROPES for step in steps]
POOL_QA = ["qa_lat_hi", "qa_lat_lo", "qa_pe_hi", "qa_pe_lo"]


class Steps:

    def __init__(self, names):
        self.names = names
        self.after = {n: i + 1 for i, n in enumerate(names)}


POOL_PRO = Steps(POOL_SETUP)
POOL_LOOP = Steps(POOL_QB + POOL_W + POOL_ROPE + POOL_QA)
POOL_LAST = Steps(POOL_QB + ["up_zero", "up_scale_zero", "down_zero", "up_scaled0", "up_scaled1", "down_scaled"])


def mla_gated_ffn_kernel(nc, x, wq, wkv_a, wkv_b, wo, kv_scale, gate_w, up_w, down_w, gate_s, up_s,
                         down_s, cos_in, sin_in, cosT_in, sinT_in, out):
    with ExitStack() as ctx:
        def sem(name):
            return ctx.enter_context(nc.semaphore(name))

        def sb(name, shape, dt=F32, where=ctx):
            return where.enter_context(nc.sbuf_tensor(name, shape, dt))

        xT_hi = sb("xT_hi", [P, KE, S], F32R)
        xT_lo = sb("xT_lo", [P, KE, S], F32R)
        acc = sb("acc", [P, NT, E])
        ident = sb("ident", [P, P])

        attn = ExitStack()

        def ab(name, shape, dt=F32):
            return sb(name, shape, dt, attn)

        lat = ab("lat", [P, S])
        pe = ab("pe", [P, S])
        q_pe = ab("q_pe", [P, BANK])
        q_swap = ab("q_swap", [P, BANK])
        cosT = ab("cosT", [P, S])
        sinT = ab("sinT", [P, S])
        QA_hi, QA_lo = ab("QA_hi", [P, S], F32R), ab("QA_lo", [P, S], F32R)
        wq_sb = ab("wq_sb", [P, KE, QW])
        wpe_hi = ab("wpe_hi", [P, KE, 2, ROPE], F32R)
        wpe_lo = ab("wpe_lo", [P, KE, 2, ROPE], F32R)
        wqT = ab("wqT", [P, 2, KE, P])
        wkv_sb = ab("wkv_sb", [LORA, KVW])
        wkvs = ab("wkvs", [P, KVW])
        wkT = ab("wkT", [P, 2, LORA])
        K_hi = [ab(f"K{h}_hi", [P, S], F32R) for h in "AB"]
        K_lo = [ab(f"K{h}_lo", [P, S], F32R) for h in "AB"]
        setup = ExitStack()

        def ub(name, shape, dt=F32):
            return sb(name, shape, dt, setup)

        wkva_sb = ub("wkva_sb", [P, KE, P])
        wkva_hi = ub("wkva_hi", [P, KE, P], F32R)
        wkva_lo = ub("wkva_lo", [P, KE, P], F32R)
        kraw = ub("kraw", [P, NT, P])
        kcat = ub("kcat", [P, NT, 3 * LORA])
        kn = ub("kn", [P, NT, LORA])
        cos_sb = ub("cos_sb", [P, NT, ROPE // 2])
        sin_sb = ub("sin_sb", [P, NT, ROPE // 2])
        sq = ub("sq", [P, BLK, LORA])
        krope_c = ub("krope_c", [P, NT, ROPE])
        krope_s = ub("krope_s", [P, NT, ROPE])
        krot = ub("krot", [P, NT, ROPE])
        stat = ub("stat", [P, NT, 6])
        mv = ub("mv", [P, NT, 2])
        var_eps = ub("var_eps", [P, NT])
        minus_half = ub("minus_half", [P, BLK])
        rstd = ub("rstd", [P, NT])
        ss = ub("ss", [P, NT])
        ms_eps = ub("ms_eps", [P, NT])
        rms = ub("rms", [P, NT])
        setup.close()
        QB_hi, QB_lo = ab("QB_hi", [P, S], F32R), ab("QB_lo", [P, S], F32R)
        Q_hi, Q_lo = [QA_hi, QB_hi], [QA_lo, QB_lo]
        prob = ab("prob", [P, NP_RING, BANK])
        pT_hi = ab("pT_hi", [P, PT_RING, BANK], F16)
        pT_lo = ab("pT_lo", [P, PT_RING, BANK], F16)
        o_raw = ab("o_raw", [P, 2, 2, VW])
        o_sum = ab("o_sum", [P, 2, 2, LORA])
        o_pair = ab("o_pair", [P, NT, P])
        oT_hi = ab("oT_hi", [P, 2, BANK], F32R)
        oT_lo = ab("oT_lo", [P, 2, BANK], F32R)
        v = ab("v", [P, NT, VW + 1], F16)
        ones = ab("ones", [P, 1])
        spare = ab("spare", [P, 1])
        wvT = ab("wvT", [P, 2, P])
        wo_sb = ab("wo_sb", [P, 2, E])
        wabs_hi = ab("wabs_hi", [P, KE, P], F32R)
        wabs_lo = ab("wabs_lo", [P, KE, P], F32R)
        wvo_hi = ab("wvo_hi", [P, E], F32R)
        wvo_lo = ab("wvo_lo", [P, E], F32R)
        scale_sb = ab("scale_sb", [LORA, 1])
        mask = ab("mask", [P, P], BF16)
        identb = ab("identb", [P, P], BF16)
        part_max = ab("part_max", [P, TILE_RING, BLK])
        neg_max = ab("neg_max", [P, TILE_RING])
        rinv = ab("rinv", [P, 2, 2])
        attn.close()

        ffn = ExitStack()

        def fb(name, shape, dt=F32):
            return sb(name, shape, dt, ffn)

        up_raw = fb("up_raw", [P, 2, IT, E])
        down_raw = fb("down_raw", [P, KE, IT * P])
        up_scale = fb("up_scale", [P, 2, IT])
        down_scale = fb("down_scale", [P, KE])
        upT_hi = fb("upT_hi", [P, 2, KE, IT * P], F32R)
        upT_lo = fb("upT_lo", [P, 2, KE, IT * P], F32R)
        downT_hi = fb("downT_hi", [P, IT, E], F32R)
        downT_lo = fb("downT_lo", [P, IT, E], F32R)
        silu_g = fb("silu_g", [P, 2, BANK])
        hid = fb("hid", [P, 2, BANK])
        hid_hi = fb("hid_hi", [P, 2, IT, BANK], F32R)
        x_in = fb("x_in", [P, NT, E])
        hid_lo = fb("hid_lo", [P, 2, IT, BANK], F32R)
        gate = fb("gate", [P, 2, 2, E])
        y = fb("y", [P, 2, 2, E])
        ffn.close()

        s_ps = ctx.enter_context(nc.psum_tensor("s_ps", [P, SBANKS, BANK], F32))
        slot_ps = ctx.enter_context(nc.psum_tensor("slot_ps", [P, 2, BANK], F32))
        o_ps = ctx.enter_context(nc.psum_tensor("o_ps", [P, BANK], F32))

        x_loaded = [sem(f"x_loaded{n}") for n in range(NG)]
        consts_loaded = sem("consts_loaded")
        wq_loaded, wkv_loaded, wo_loaded = sem("wq_loaded"), sem("wkv_loaded"), sem("wo_loaded")
        slot_ready, hi_done = sem("slot_ready"), sem("hi_done")
        act_freed, dve_freed = sem("act_freed"), sem("dve_freed")
        pool_done = sem("pool_done")
        dve_setup = sem("dve_setup")
        xn_done = sem("xn_done")
        kcat_done = sem("kcat_done")
        wkva_done = sem("wkva_done")
        scores_ready = sem("scores_ready")
        part_done = sem("part_done")
        max_ready = sem("max_ready")
        exp_done = sem("exp_done")
        pv_done = sem("pv_done")

        tables_loaded = sem("tables_loaded")
        swapped = sem("swapped")
        var_ready = sem("var_ready")
        ms_ready = sem("ms_ready")
        queries_split = sem("queries_split")
        o_copied = sem("o_copied")
        summed = sem("summed")
        norm_done = sem("norm_done")
        ffn_loaded = sem("ffn_loaded")
        gu_ready, silu_done, hid_done = sem("gu_ready"), sem("silu_done"), sem("hid_done")
        hid_hi_done, hid_lo_done = sem("hid_hi_done"), sem("hid_lo_done")
        down_ready, gate_done = sem("down_ready"), sem("gate_done")
        gated, y_done = sem("gated"), sem("y_done")
        stored = [sem("stored0"), sem("stored1")]
        x_again = sem("x_again")

        setup_ph = Phase(SETUP, POOL_PRO, {"ready": 0, "hi": 0, "act": 0, "dve": 0}, 0)
        loop_ph = Phase(LOOP, POOL_LOOP, setup_ph.end(), len(POOL_PRO.names))
        last_ph = Phase(LAST, POOL_LAST, loop_ph.end(PAIRS - 1),
                        loop_ph.pool_base + (PAIRS - 1) * len(POOL_LOOP.names), PAIRS - 1)
        tail_ph = Phase(TAIL, None, last_ph.end(), 0)
        PARTS = sum(not (c[4] and c[5]) for c in CHUNKS) * 2
        part_of = {}
        for g in range(STEPS):
            first, last = chunk(g)[5:]
            part_of[g] = len([i for i in part_of.values() if i]) + 1 if not (first and last) else 0

        def setup_bank(i):
            i %= SETUP_BANKS
            return slot_ps[:, i, :] if i < 2 else s_ps[:, i - 2, :]

        block = ctx.enter_context(nc.Block())

        @block.sync
        def _(sp):
            xv = x[0].rearrange("(t p) d -> p t d", p=P)
            for n in range(NG):
                sp.dma_start(acc[:, BLK * n:BLK * n + BLK, :], xv[:, BLK * n:BLK * n + BLK, :]).then_inc(x_loaded[n], 16)

            def load(pair):
                wqv = wq.rearrange("(k e) n -> e k n", k=KE)
                sp.dma_start(wq_sb[:], wqv[:, :, bass.ds(pair * QW, QW)]).then_inc(wq_loaded, 16)
                sp.dma_start(wkv_sb[:], wkv_b[:, bass.ds(pair * KVW, KVW)]).then_inc(wkv_loaded, 16)

            def load_wo(pair):
                wov = wo.rearrange("(h d) n -> d h n", d=VD)
                sp.dma_start(wo_sb[:], wov[:, bass.ds(pair * 2, 2), :]).then_inc(wo_loaded, 16)

            load(0)
            load_wo(0)
            with sp.Fori(0, PAIRS - 1) as p:
                ph = loop_ph.of_pair(p)
                sp.wait_ge(slot_ready, ph.base["ready"])
                sp.wait_ge(pool_done, ph.pool_base)
                load(p + 1)
                sp.wait_ge(slot_ready, ph.after("ready", "wvo"))
                load_wo(p + 1)

            sp.wait_ge(slot_ready, last_ph.base["ready"])
            sp.wait_ge(pool_done, last_ph.pool_after("down_zero"))
            whole = INTER // P
            rest = INTER - whole * P
            for w, src in enumerate((gate_w, up_w)):
                sp.dma_start(up_raw[:, w, 0:whole, :], src[0:whole * P, :].rearrange("(t p) e -> p t e", p=P)).then_inc(ffn_loaded, 16)
                sp.dma_start(up_raw[0:rest, w, whole, :], src[whole * P:INTER, :]).then_inc(ffn_loaded, 16)
            for w, src in enumerate((gate_s, up_s)):
                with nc.allow_non_contiguous_dma(reason="scales, one value to a partition"):
                    sp.dma_start(up_scale[:, w, 0:whole], src[0:whole * P].rearrange("(t p) -> p t", p=P)).then_inc(ffn_loaded, 16)
                    sp.dma_start(up_scale[0:rest, w, whole:whole + 1], src[whole * P:INTER].rearrange("(p o) -> p o", o=1)).then_inc(ffn_loaded, 16)
            sp.dma_start(down_raw[:, :, 0:INTER], down_w.rearrange("(k p) i -> p k i", p=P)).then_inc(ffn_loaded, 16)
            with nc.allow_non_contiguous_dma(reason="scales, one value to a partition"):
                sp.dma_start(down_scale[:], down_s.rearrange("(k p) -> p k", p=P)).then_inc(ffn_loaded, 16)
            sp.wait_ge(scores_ready, PAIRS * STEPS)
            sp.dma_start(x_in[:], xv).then_inc(x_again, 16)
            yv = out[0].rearrange("(t p) d -> p t d", p=P)
            for u in range(2 * NG):
                sp.wait_ge(y_done, u + 1)
                sp.dma_start(yv[:, 2 * u:2 * u + 2, :], y[:, u % 2]).then_inc(stored[u % 2], 16)
            for done in stored:
                sp.wait_ge(done, 16 * NG)

        @block.tensor
        def _(pe_eng):
            def slot(ph, name):
                i = ph.slots.at[name]
                if ph is setup_ph:
                    if i >= SETUP_BANKS:
                        freed = "act" if ph.slots.kinds[i - SETUP_BANKS] == BY_ACT else "dve"
                        pe_eng.wait_ge(act_freed if freed == "act" else dve_freed, ph.slots.counts[i - SETUP_BANKS][freed])
                    return setup_bank(i)
                if i >= 2:
                    freed = "act" if ph.slots.kinds[i - 2] == BY_ACT else "dve"
                    pe_eng.wait_ge(act_freed if freed == "act" else dve_freed,
                                   ph.base[freed] + ph.slots.counts[i - 2][freed])
                elif i == 0:
                    pe_eng.wait_ge(act_freed, ph.base["act"])
                    pe_eng.wait_ge(dve_freed, ph.base["dve"])
                return slot_ps[:, i % 2, :]

            def exact(out_ap, parts):
                n = 3 * len(parts)
                i = 0
                for a_hi, a_lo, b_hi, b_lo in parts:
                    for a, b in ((a_hi, b_hi), (a_hi, b_lo), (a_lo, b_hi)):
                        last = nc.tensor.matmul(out_ap, a, b, start=(i == 0), stop=(i == n - 1))
                        i += 1
                return last

            def x_tile(t):
                return [(xT_hi[:, k, t * P:(t + 1) * P], xT_lo[:, k, t * P:(t + 1) * P]) for k in range(KE)]

            def prep_job(ph, name, pair_after):
                ps = slot(ph, name)
                if name == "wqT":
                    pe_eng.wait_ge(wq_loaded, 16 * pair_after)
                    for h in range(2):
                        for k in range(KE):
                            c = h * (NOPE + ROPE)
                            last = nc.tensor.transpose(ps[:, (h * KE + k) * P:(h * KE + k + 1) * P], wq_sb[:, k, c:c + NOPE], ident[:])
                elif name == "wkvT":
                    pe_eng.wait_ge(pool_done, ph.pool_after("wkvs"))
                    for i in range(4):
                        last = nc.tensor.transpose(ps[:, i * P:(i + 1) * P], wkvs[:, i * P:(i + 1) * P], ident[:])
                elif name == "wabs":
                    pe_eng.wait_ge(act_freed, ph.after("act", "wkvT"))
                    for k in range(KE):
                        for h in (1, 0):
                            c = k * P + (1 - h) * LORA
                            last = nc.tensor.matmul(ps[:, c:c + LORA], wqT[:, h, k, :], wkT[:, h, :], start=True, stop=True)
                elif name.startswith("lat"):
                    pe_eng.wait_ge(dve_freed, ph.after("dve", "wabs"))
                    c = query_cols(int(name[3:]))
                    last = exact(ps, [(wabs_hi[:, k, :], wabs_lo[:, k, :], xT_hi[:, k, c], xT_lo[:, k, c]) for k in range(KE)])
                else:
                    pe_eng.wait_ge(pool_done, ph.pool_after("wpe_lo"))
                    c = query_cols(int(name[2:]))
                    last = exact(ps, [(wpe_hi[:, k, :, :].rearrange("p h c -> p (h c)"), wpe_lo[:, k, :, :].rearrange("p h c -> p (h c)"),
                                       xT_hi[:, k, c], xT_lo[:, k, c]) for k in range(KE)])
                last.then_inc(slot_ready, 1)

            def out_job(ph, name, pair):
                if name == "wvo":
                    ps = slot(ph, name)
                    pe_eng.wait_ge(wo_loaded, 16 * (pair + 1))
                    for h in range(2):
                        last = nc.tensor.matmul(ps[:, 0:E], wvT[:, h, :], wo_sb[:, h, :], start=(h == 0), stop=(h == 1))
                    last.then_inc(slot_ready, 1)
                    return
                q = int(name[4])
                if name.startswith("outT"):
                    ps = slot(ph, name)
                    done = 1 + NT * pair if q == NG - 1 else 1 + NT * pair + NT // 2 + 2 * q + 2
                    pe_eng.wait_ge(norm_done, done)
                    for j in range(BLK):
                        last = nc.tensor.transpose(ps[:, j * P:(j + 1) * P], o_pair[:, TILE_ORDER[4 * q + j], :], ident[:])
                else:
                    half = "ab".index(name[5])
                    ps = slot(ph, name)
                    pe_eng.wait_ge(dve_freed, ph.after("dve", f"outT{q}"))
                    for i, j in enumerate((2 * half + 1, 2 * half)):
                        c = slice(j * P, (j + 1) * P)
                        last = exact(ps[:, i * E:(i + 1) * E], [(oT_hi[:, q % 2, c], oT_lo[:, q % 2, c], wvo_hi[:], wvo_lo[:])])
                last.then_inc(slot_ready, 1)

            def scores(g, queries_ready):
                head, t, _, k0, w, first, last_chunk = chunk(g)
                if g % NCH == 0 and queries_ready is not None:
                    pe_eng.wait_ge(pool_done, queries_ready)
                out_ap = s_ps[:, g % SBANKS, 0:w]
                q = slice(t * P, (t + 1) * P)
                for i, (a, b) in enumerate(((Q_hi, K_hi), (Q_hi, K_lo), (Q_lo, K_hi))):
                    mm = nc.tensor.matmul(out_ap, a[head][:, q], b[head][:, k0:k0 + w],
                                          start=(i == 0), stop=(i == 2 and not last_chunk))
                if last_chunk:
                    mm = nc.tensor.matmul(out_ap[:, w - P:w], identb[:], mask[:], start=False, stop=True)
                mm.then_inc(scores_ready, 1)

            def turn(ph, g):
                ps = slot(ph, ("T", g))
                pe_eng.wait_ge(exp_done, ph.pair * STEPS + g + 1)
                for b in range(chunk(g)[4] // P):
                    last = nc.tensor.transpose(ps[:, b * P:(b + 1) * P], prob[:, g % NP_RING, b * P:(b + 1) * P], ident[:])
                last.then_inc(slot_ready, 1)

            def weigh(ph, g):
                _, _, tile_no, k0, w, first, last_chunk = chunk(g)
                pe_eng.wait_ge(dve_freed, ph.after("dve", ("T", g)))
                if g % SBANKS == 0:
                    pe_eng.wait_ge(o_copied, 1 + ph.pair * NT + g // SBANKS)
                c0 = tile_no % 2 * VW
                n = w // P
                for b in range(n):
                    kb = k0 // P + b
                    c = slice(b * P, (b + 1) * P)
                    hi, lo = pT_hi[:, g % PT_RING, c], pT_lo[:, g % PT_RING, c]
                    nc.tensor.matmul(o_ps[:, c0:c0 + VW], hi, v[:, kb, 0:VW], start=(first and b == 0), stop=False)
                    last = nc.tensor.matmul(o_ps[:, c0:c0 + LORA + 1], lo, v[:, kb, 0:LORA + 1], start=False, stop=(last_chunk and b == n - 1))
                last.then_inc(pv_done, 1)

            def ffn_job(ph, name):
                ps = slot(ph, name)
                if name == FFN_UP[0]:
                    pe_eng.wait_ge(pool_done, ph.pool_after("down_scaled"))
                if name in FFN_UP:
                    w, k, half = name
                    for j in range(IT // 2):
                        last = nc.tensor.transpose(ps[:, j * P:(j + 1) * P], up_raw[:, w, half * (IT // 2) + j, k * P:(k + 1) * P], ident[:])
                else:
                    for j in range(2):
                        for k in range(KE):
                            c = (2 * name[1] + j) * P
                            last = nc.tensor.transpose(ps[:, j * E + k * P:j * E + (k + 1) * P], down_raw[:, k, c:c + P], ident[:])
                last.then_inc(slot_ready, 1)

            def job(ph, name):
                if name in FFN_UP + FFN_DOWN:
                    ffn_job(ph, name)
                elif name.startswith("out") or name == "wvo":
                    out_job(ph, name, ph.pair)
                else:
                    prep_job(ph, name, ph.pair + 2)

            def pair_program(ph, jobs, prep):
                for s in range(STEPS):
                    for part in PE_STEP[s % SBANKS]:
                        if part == "turn":
                            turn(ph, s)
                        elif part == "scores" and s + SBANKS < STEPS:
                            scores(s + SBANKS, ph.pool_after("qb_pe_lo"))
                        elif part == "scores" and prep:
                            scores(s + SBANKS, ph.pool_after("qa_pe_lo"))
                        elif part == "job" and s in jobs:
                            job(ph, jobs[s][0])
                        elif part == "weigh":
                            for g in weigh_at(s):
                                weigh(ph, g)
                for g in WEIGH_END:
                    weigh(ph, g)

            def setup_job(ph, name):
                ps = slot(ph, name)
                n = name[1]
                if name[0] == "xT":
                    k = name[2]
                    pe_eng.wait_ge(xn_done, BLK * (n + 1))
                    for j in range(BLK):
                        last = nc.tensor.transpose(ps[:, j * P:(j + 1) * P], acc[:, BLK * n + j, k * P:(k + 1) * P], ident[:])
                elif name[0] == "kv":
                    pe_eng.wait_ge(wkva_done, 2)
                    pe_eng.wait_ge(dve_freed, ph.after("dve", ("xT", n, KE - 1)))
                    for j in range(BLK):
                        last = exact(ps[:, j * P:(j + 1) * P], [(*a, wkva_hi[:, k, :], wkva_lo[:, k, :]) for k, a in enumerate(x_tile(BLK * n + j))])
                else:
                    c = 0 if name[2] == "B" else LORA
                    pe_eng.wait_ge(kcat_done, n + 1)
                    pe_eng.wait_ge(pool_done, ph.pool_after(f"kr{n}.5"))
                    for j in range(BLK):
                        last = nc.tensor.transpose(ps[:, j * P:(j + 1) * P], kcat[:, BLK * n + j, c:c + P], ident[:])
                last.then_inc(slot_ready, 1)

            ph = setup_ph
            pe_eng.wait_ge(pool_done, ph.pool_after("ident"))
            for _ in range(WARM_UP):
                nc.tensor.transpose(o_ps[:, 0:P], ident[:], ident[:])
            for name in SETUP_ORDER:
                if isinstance(name, tuple):
                    setup_job(ph, name)
                else:
                    prep_job(ph, name, 1)
            pe_eng.wait_ge(queries_split, 1)
            pe_eng.wait_ge(dve_freed, ph.slots.count["dve"])
            for g in range(SBANKS):
                scores(g, None)
            pe_eng.wait_ge(queries_split, 2)
            with pe_eng.Fori(0, PAIRS - 1) as p:
                pair_program(loop_ph.of_pair(p), LOOP_JOBS, True)
            pair_program(last_ph, LAST_JOBS, False)
            ph = tail_ph

            def gate_up(n):
                for it in range(IT):
                    j = n * IT + it
                    if j >= 2:
                        pe_eng.wait_ge(hid_done, j - 1)
                    if j == 0:
                        pe_eng.wait_ge(dve_freed, last_ph.after("dve", FFN_DOWN[-1]))
                    c = slice(n * BANK, (n + 1) * BANK)
                    i = slice(it * P, (it + 1) * P)
                    for w in range(2):
                        last = exact(s_ps[:, 2 * (j % 2) + w, :], [
                            (upT_hi[:, w, k, i], upT_lo[:, w, k, i], xT_hi[:, k, c], xT_lo[:, k, c]) for k in range(KE)])
                    last.then_inc(gu_ready, 1)
                    if j < len(OUT_LAST):
                        out_job(tail_ph, OUT_LAST[j][0], PAIRS)

            def down(n):
                pe_eng.wait_ge(hid_lo_done, IT * (n + 1))
                for tp in range(2):
                    u = 2 * n + tp
                    if u >= 2:
                        pe_eng.wait_ge(gate_done, u - 1)
                    for j in range(2):
                        c = slice((2 * tp + j) * P, (2 * tp + j + 1) * P)
                        bank = s_ps[:, SBANKS - 1, :] if u % 2 else o_ps[:, :]
                        last = exact(bank[:, j * E:(j + 1) * E], [
                            (hid_hi[:, n % 2, it, c], hid_lo[:, n % 2, it, c], downT_hi[:, it, :], downT_lo[:, it, :]) for it in range(IT)])
                    last.then_inc(down_ready, 1)

            gate_up(0)
            for n in range(1, NG):
                gate_up(n)
                down(n - 1)
            down(NG - 1)

        @block.scalar
        def _(act):
            def copy(dst, src):
                return nc.scalar.activation(dst, src, ACT.Copy)

            def slot_of(ph, name):
                act.wait_ge(slot_ready, ph.after("ready", name))
                if ph is setup_ph:
                    return setup_bank(ph.slots.at[name])
                return slot_ps[:, ph.slots.at[name] % 2, :]

            def prep_job(ph, name):
                ps = slot_of(ph, name)
                if name == "wqT":
                    copy(wqT[:].rearrange("p h k e -> p (h k e)"), ps).then_inc(act_freed, 1)
                elif name == "wkvT":
                    blocks = ps.rearrange("p (h v c) -> p h v c", h=2, v=2)
                    copy(wkT[:], blocks[:, :, 0, 0:LORA])
                    copy(wvT[:, 0, 0:LORA], blocks[:, 0, 1, 0:LORA])
                    copy(wvT[:, 1, LORA:P], blocks[:, 1, 1, 0:LORA]).then_inc(act_freed, 1)
                elif name == "wabs":
                    copy(wabs_hi[:].rearrange("p k c -> p (k c)"), ps[:, 0:KE * P]).then_inc(hi_done, 1)
                elif name.startswith("lat"):
                    if ph is not setup_ph:
                        act.wait_ge(pool_done, ph.pool_after("qb_pe_lo"))
                    copy(lat[:, query_cols(int(name[3:]))], ps).then_inc(act_freed, 1)
                else:
                    n = int(name[2:])
                    if n >= 1:
                        act.wait_ge(pool_done, ph.pool_after(f"rope{n - 1}.0"))
                    copy(q_pe[:], ps).then_inc(act_freed, 1)

            def out_job(ph, name):
                if name == "wvo":
                    copy(wvo_hi[:], slot_of(ph, name)[:, 0:E]).then_inc(hi_done, 1)
                elif name.startswith("outT"):
                    copy(oT_hi[:, int(name[4]) % 2, :], slot_of(ph, name)).then_inc(hi_done, 1)

            def exponentials(pair, g):
                _, _, tile_no, _, w, first, _ = chunk(g)
                if first:
                    act.wait_ge(max_ready, (pair + g // STEPS) * 2 * NT + tile_no + 1)
                nc.scalar.activation(prob[:, g % STEPS % NP_RING, 0:w], s_ps[:, g % SBANKS, 0:w], ACT.Exp,
                                     bias=neg_max[:, tile_no % TILE_RING:tile_no % TILE_RING + 1]).then_inc(exp_done, 1)

            def copy_outputs(ph, r):
                act.wait_ge(pv_done, ph.pair * STEPS + SBANKS * (r + 1))
                copy(o_raw[:, r % 2].rearrange("p t c -> p (t c)"), o_ps[:, 0:2 * VW]).then_inc(o_copied, 1)

            def turned_hi(ph, g):
                w = chunk(g)[4]
                copy(pT_hi[:, g % PT_RING, 0:w], slot_of(ph, ("T", g))[:, 0:w]).then_inc(hi_done, 1)

            def ffn_job(ph, name):
                ps = slot_of(ph, name)
                if name == FFN_UP[0]:
                    act.wait_ge(scores_ready, ph.pair * STEPS + NCH)
                if name in FFN_UP:
                    w, k, half = name
                    c = IT // 2 * P
                    copy(upT_hi[:, w, k, half * c:(half + 1) * c], ps[:, 0:c]).then_inc(hi_done, 1)
                else:
                    i = name[1]
                    copy(downT_hi[:, 2 * i:2 * i + 2, :].rearrange("p t e -> p (t e)"), ps).then_inc(hi_done, 1)

            def job(ph, name):
                if name in FFN_UP + FFN_DOWN:
                    ffn_job(ph, name)
                elif name.startswith("out") or name == "wvo":
                    out_job(ph, name)
                else:
                    prep_job(ph, name)

            def pair_program(ph, jobs, prep):
                for s in range(STEPS):
                    for part in ACT_STEP[s % SBANKS]:
                        if part == "exp" and (s + 1 < STEPS or prep):
                            exponentials(ph.pair, s + 1)
                        elif part == "hi":
                            turned_hi(ph, s)
                        elif part == "outputs" and s > SBANKS:
                            copy_outputs(ph, s // SBANKS - 1)
                        elif part == "job" and s in jobs:
                            job(ph, jobs[s][0])
                copy_outputs(ph, STEPS // SBANKS - 1)

            act.dma_start(wkva_sb[:], wkv_a.rearrange("(k e) c -> e k c", k=KE)).then_inc(consts_loaded, 16)
            act.dma_start(cos_sb[:], cos_in.rearrange("(t p) d -> p t d", p=P)).then_inc(consts_loaded, 16)
            act.dma_start(sin_sb[:], sin_in.rearrange("(t p) d -> p t d", p=P)).then_inc(consts_loaded, 16)
            act.dma_start(scale_sb[:], kv_scale.rearrange("(l o) -> l o", o=1)).then_inc(consts_loaded, 16)
            act.dma_start(cosT[:], cosT_in).then_inc(tables_loaded, 16)
            act.dma_start(sinT[:], sinT_in).then_inc(tables_loaded, 16)
            ph = setup_ph
            for name in SETUP_ORDER:
                if name[0] == "xT":
                    _, n, k = name
                    copy(xT_hi[:, k, n * BANK:(n + 1) * BANK], slot_of(ph, name)).then_inc(hi_done, 1)
                elif name[0] == "kv":
                    n = name[1]
                    copy(kraw[:, BLK * n:BLK * n + BLK, :].rearrange("p t c -> p (t c)"), slot_of(ph, name)).then_inc(act_freed, 1)
                elif name[0] == "K":
                    _, n, side = name
                    copy(K_hi["AB".index(side)][:, n * BANK:(n + 1) * BANK], slot_of(ph, name)).then_inc(hi_done, 1)
                else:
                    prep_job(ph, name)
            copy(spare[:], ones[:]).then_inc(o_copied, 1)
            exponentials(0, 0)
            with act.Fori(0, PAIRS - 1) as p:
                pair_program(loop_ph.of_pair(p), LOOP_JOBS, True)
            pair_program(last_ph, LAST_JOBS, False)
            def hidden_hi(j):
                n, it = divmod(j, IT)
                act.wait_ge(hid_done, j + 1)
                if n >= 2:
                    act.wait_ge(down_ready, 2 * (n - 1))
                copy(hid_hi[:, n % 2, it, :], hid[:, j % 2, :]).then_inc(hid_hi_done, 1)

            def out_gate(u):
                act.wait_ge(down_ready, u + 1)
                if u >= 2:
                    act.wait_ge(gated, u - 1)
                bank = s_ps[:, SBANKS - 1, :] if u % 2 else o_ps[:, :]
                nc.scalar.activation(gate[:, u % 2].rearrange("p t e -> p (t e)"), bank, ACT.Silu).then_inc(gate_done, 1)

            for j in range(NG * IT):
                act.wait_ge(gu_ready, j + 1)
                if j >= 2:
                    act.wait_ge(hid_done, j - 1)
                nc.scalar.activation(silu_g[:, j % 2, :], s_ps[:, 2 * (j % 2), :], ACT.Silu).then_inc(silu_done, 1)
                if j < len(OUT_LAST):
                    out_job(tail_ph, OUT_LAST[j][0])
                if j >= 1:
                    hidden_hi(j - 1)
                if j % IT == 3 and j >= 2 * IT:
                    out_gate(2 * (j // IT) - 4)
                    out_gate(2 * (j // IT) - 3)
            hidden_hi(NG * IT - 1)
            for u in range(2 * NG - 4, 2 * NG):
                out_gate(u)

        @block.vector
        def _(dve):
            steps = [0]

            def then_wait(instruction):
                steps[0] += 1
                instruction.then_inc(dve_setup, 1)
                dve.wait_ge(dve_setup, steps[0])

            def lo_of(ph, name, dst, hi, cols=slice(0, BANK)):
                dve.wait_ge(hi_done, ph.after("hi", name))
                i = ph.slots.at[name]
                ps = setup_bank(i)[:, cols] if ph is setup_ph else slot_ps[:, i % 2, cols]
                nc.vector.tensor_tensor(dst, ps, hi, ALU.subtract).then_inc(dve_freed, 1)

            def f32(ap):
                return ap.bitcast(F32)

            def out_job(ph, name):
                if name == "wvo":
                    lo_of(ph, name, wvo_lo[:], f32(wvo_hi[:]), slice(0, E))
                    return
                q = int(name[4])
                if name.startswith("outT"):
                    lo_of(ph, name, oT_lo[:, q % 2, :], f32(oT_hi[:, q % 2, :]))
                    return
                half = "ab".index(name[5])
                high, low = TILE_ORDER[4 * q + 2 * half:4 * q + 2 * half + 2]
                tiles = acc[:, low:high + 1:high - low, :]
                dve.wait_ge(slot_ready, ph.after("ready", name))
                ps = slot_ps[:, ph.slots.at[name] % 2, :].rearrange("p (t e) -> p t e", t=2)
                nc.vector.tensor_tensor(tiles, ps, tiles, ALU.add).then_inc(dve_freed, 1)

            def row_max(pair, g):
                _, _, tile_no, k0, w, first, last_chunk = chunk(g)
                pair = pair + g // STEPS
                g %= STEPS
                r = tile_no % TILE_RING
                c = k0 // BANK
                dve.wait_ge(scores_ready, pair * STEPS + g + 1)
                src = s_ps[:, g % SBANKS, 0:w]
                if first and last_chunk:
                    nc.vector.tensor_reduce(neg_max[:, r:r + 1], src, AX.X, ALU.max, negate=True).then_inc(max_ready, 1)
                    return
                nc.vector.tensor_reduce(part_max[:, r, c:c + 1], src, AX.X, ALU.max).then_inc(part_done, 1)
                if last_chunk:
                    dve.wait_ge(part_done, pair * PARTS + part_of[g])
                    nc.vector.tensor_reduce(neg_max[:, r:r + 1], part_max[:, r, 0:c + 1], AX.X, ALU.max, negate=True).then_inc(max_ready, 1)

            def normalise(ph, r):
                head, high = chunk(SBANKS * r)[:2]
                low = NT - 1 - high
                b = r % 2
                done = ph.pair * NT + r + 1
                dve.wait_ge(o_copied, 1 + done)
                nc.vector.tensor_tensor(o_sum[:, b], o_raw[:, b, :, 0:LORA], o_raw[:, b, :, LORA + 1:VW], ALU.add)
                nc.vector.reciprocal(rinv[:, b, :], o_raw[:, b, :, LORA]).then_inc(summed, 1)
                dve.wait_ge(summed, done)
                nc.vector.tensor_tensor(o_pair[:, high:(low - 1 if low else None):low - high, head * LORA:(head + 1) * LORA], o_sum[:, b],
                                        rinv[:, b, :].unsqueeze(2).to_broadcast([P, 2, LORA]), ALU.mult).then_inc(norm_done, 1)

            def ffn_job(ph, name):
                if name in FFN_UP:
                    w, k, half = name
                    c = slice(half * (IT // 2 * P), (half + 1) * (IT // 2 * P))
                    lo_of(ph, name, upT_lo[:, w, k, c], f32(upT_hi[:, w, k, c]), slice(0, IT // 2 * P))
                else:
                    tiles = slice(2 * name[1], 2 * name[1] + 2)
                    lo_of(ph, name, downT_lo[:, tiles, :].rearrange("p t e -> p (t e)"), f32(downT_hi[:, tiles, :].rearrange("p t e -> p (t e)")))

            def job(ph, name):
                if name in FFN_UP + FFN_DOWN:
                    ffn_job(ph, name)
                elif name.startswith("out") or name == "wvo":
                    out_job(ph, name)
                elif name == "wabs":
                    lo_of(ph, name, wabs_lo[:].rearrange("p k c -> p (k c)"), f32(wabs_hi[:].rearrange("p k c -> p (k c)")), slice(0, KE * P))

            def swap(ph, n, head):
                dve.wait_ge(act_freed, ph.after("act", f"pe{n}"))
                if n >= 1 and head == 0:
                    dve.wait_ge(pool_done, ph.pool_after(f"rope{n - 1}.2"))
                half = ROPE // 2
                x1, x2 = slice(head * ROPE, head * ROPE + half), slice(head * ROPE + half, (head + 1) * ROPE)
                nc.vector.tensor_copy(q_swap[x1, :], q_pe[x2, :])
                last = nc.vector.tensor_copy(q_swap[x2, :], q_pe[x1, :])
                if head == 1:
                    last.then_inc(swapped, 1)

            def pair_program(ph, jobs, prep):
                for s in range(STEPS):
                    for part in DVE_STEP[s % SBANKS]:
                        if part == "max" and (s + SBANKS < STEPS or prep):
                            row_max(ph.pair, s + SBANKS)
                        elif part == "lo":
                            w = chunk(s)[4]
                            lo_of(ph, ("T", s), pT_lo[:, s % PT_RING, 0:w], pT_hi[:, s % PT_RING, 0:w], slice(0, w))
                        elif part == "normalise" and s > SBANKS:
                            normalise(ph, s // SBANKS - 1)
                        elif part == "job" and s in jobs:
                            job(ph, jobs[s][0])
                    for head in range(2):
                        if jobs.get(s - 1 - head, ("",))[0] in QUERY_JOBS:
                            swap(ph, QUERY_JOBS.index(jobs[s - 1 - head][0]), head)
                normalise(ph, STEPS // SBANKS - 1)

            def stats(n):
                dve.wait_ge(x_loaded[n], 16)
                for t in range(BLK * n, BLK * n + BLK):
                    last = nc.vector.bn_stats(stat[:, t, :], acc[:, t, :])
                then_wait(last)
                for t in range(BLK * n, BLK * n + BLK):
                    last = nc.vector.bn_aggr(mv[:, t, :], stat[:, t, :])
                then_wait(last)
                nc.vector.tensor_scalar(var_eps[:, BLK * n:BLK * n + BLK], mv[:, BLK * n:BLK * n + BLK, 1], EPS_LN, None, ALU.add).then_inc(var_ready, 1)

            ph = setup_ph

            def normalise_x(n):
                dve.wait_ge(pool_done, ph.pool_after(f"rstd{n}"))
                for t in range(BLK * n, BLK * n + BLK):
                    nc.vector.tensor_scalar(acc[:, t, :], acc[:, t, :], mv[:, t, 0:1], rstd[:, t:t + 1],
                                            ALU.subtract, ALU.mult).then_inc(xn_done, 1)

            def x_lo(n):
                for k in range(KE):
                    c = slice(n * BANK, (n + 1) * BANK)
                    lo_of(ph, ("xT", n, k), xT_lo[:, k, c], f32(xT_hi[:, k, c]))

            def squares(n):
                tiles = slice(BLK * n, BLK * n + BLK)
                ckv = kraw[:, tiles, 0:LORA]
                dve.wait_ge(act_freed, ph.after("act", ("kv", n)))
                then_wait(nc.vector.tensor_tensor(sq[:], ckv, ckv, ALU.mult))
                then_wait(nc.vector.tensor_reduce(ss[:, tiles], sq[:], AX.X, ALU.add))
                nc.vector.tensor_scalar(ms_eps[:, tiles], ss[:, tiles], 1.0 / LORA, EPS_RMS, ALU.mult, ALU.add).then_inc(ms_ready, 1)

            def values_and_keys(n):
                tiles = slice(BLK * n, BLK * n + BLK)
                dve.wait_ge(pool_done, ph.pool_after(f"rms{n}"))
                then_wait(nc.vector.tensor_tensor(kn[:, tiles, :], kraw[:, tiles, 0:LORA],
                                                  rms[:, tiles].unsqueeze(2).to_broadcast([P, BLK, LORA]), ALU.mult))
                then_wait(nc.vector.tensor_copy(v[:, tiles, 0:LORA], kn[:, tiles, :]))
                nc.vector.tensor_tensor(v[:, tiles, LORA + 1:VW], kn[:, tiles, :], v[:, tiles, 0:LORA], ALU.subtract)
                nc.vector.tensor_scalar(kcat[:, tiles, 0:LORA], kn[:, tiles, :], SCALE, None, ALU.mult)
                nc.vector.tensor_scalar(kcat[:, tiles, 2 * LORA:3 * LORA], kn[:, tiles, :], SCALE, None, ALU.mult).then_inc(kcat_done, 1)

            def keys_lo(n):
                c = slice(n * BANK, (n + 1) * BANK)
                for i, side in ((1, "B"), (0, "A")):
                    lo_of(ph, ("K", n, side), K_lo[i][:, c], f32(K_hi[i][:, c]))

            def split_queries(n):
                c = query_cols(n)
                dve.wait_ge(act_freed, ph.after("act", f"lat{n}"))
                dve.wait_ge(pool_done, ph.pool_after(f"rope{n}.2"))
                nc.vector.tensor_copy(QA_hi[LORA:P, c], lat[LORA:P, c])
                then_wait(nc.vector.tensor_copy(QA_hi[0:LORA, c], pe[0:LORA, c]))
                nc.vector.tensor_tensor(QA_lo[LORA:P, c], lat[LORA:P, c], f32(QA_hi[LORA:P, c]), ALU.subtract)
                return nc.vector.tensor_tensor(QA_lo[0:LORA, c], pe[0:LORA, c], f32(QA_hi[0:LORA, c]), ALU.subtract)

            def swap_both(n):
                swap(ph, n, 0)
                swap(ph, n, 1)

            stats(0)
            stats(1)
            normalise_x(0)
            normalise_x(1)
            dve.wait_ge(consts_loaded, 64)
            nc.vector.tensor_copy(wkva_hi[:], wkva_sb[:]).then_inc(wkva_done, 1)
            dve.wait_ge(wkva_done, 1)
            nc.vector.tensor_tensor(wkva_lo[:], wkva_sb[:], f32(wkva_hi[:]), ALU.subtract).then_inc(wkva_done, 1)
            stats(2)
            x_lo(0)
            normalise_x(2)
            stats(3)
            x_lo(1)
            normalise_x(3)
            squares(0)
            x_lo(2)
            values_and_keys(0)
            squares(1)
            x_lo(3)
            swap_both(0)
            values_and_keys(1)
            squares(2)
            lo_of(ph, "wabs", wabs_lo[:].rearrange("p k c -> p (k c)"), f32(wabs_hi[:].rearrange("p k c -> p (k c)")), slice(0, KE * P))
            squares(3)
            nc.vector.memset(f32(wvo_hi[:]), 0.0)
            nc.vector.memset(acc[:, 0:NT // 2, :], 0.0)
            keys_lo(0)
            swap_both(1)
            values_and_keys(2)
            nc.vector.memset(acc[:, NT // 2:NT, :], 0.0)
            keys_lo(1)
            values_and_keys(3)
            swap_both(2)
            keys_lo(2)
            split_queries(0)
            split_queries(1).then_inc(queries_split, 1)
            keys_lo(3)
            swap_both(3)
            split_queries(2)
            nc.vector.memset(o_pair[:, min(TILE_ORDER[-BLK:]):max(TILE_ORDER[-BLK:]) + 1, :], 0.0)
            nc.vector.memset(f32(wvo_lo[:]), 0.0).then_inc(norm_done, 1)
            for g in range(SBANKS):
                row_max(0, g)
            split_queries(3).then_inc(queries_split, 1)
            with dve.Fori(0, PAIRS - 1) as p:
                pair_program(loop_ph.of_pair(p), LOOP_JOBS, True)
            pair_program(last_ph, LAST_JOBS, False)
            def finish(u):
                tiles = slice(2 * u, 2 * u + 2)
                dve.wait_ge(gate_done, u + 1)
                if u >= 2:
                    dve.wait_ge(stored[u % 2], 16 * (u // 2))
                nc.vector.tensor_tensor(y[:, u % 2], gate[:, u % 2], acc[:, tiles, :], ALU.mult).then_inc(gated, 1)
                dve.wait_ge(gated, u + 1)
                if u == 0:
                    dve.wait_ge(x_again, 16)
                nc.vector.tensor_tensor(y[:, u % 2], y[:, u % 2], x_in[:, tiles, :], ALU.add).then_inc(y_done, 1)

            for j in range(NG * IT):
                dve.wait_ge(silu_done, j + 1)
                if j >= 2:
                    dve.wait_ge(hid_lo_done, j - 1)
                nc.vector.tensor_tensor(hid[:, j % 2, :], s_ps[:, 2 * (j % 2) + 1, :], silu_g[:, j % 2, :], ALU.mult).then_inc(hid_done, 1)
                if j < len(OUT_LAST):
                    out_job(tail_ph, OUT_LAST[j][0])
                if j % IT == 4 and j >= 2 * IT:
                    finish(2 * (j // IT) - 4)
                    finish(2 * (j // IT) - 3)
            for u in range(2 * NG - 4, 2 * NG):
                finish(u)

        @block.gpsimd
        def _(pool):
            def run(ph, name, issue, *waits):
                value = ph.pool_after(name)
                if ph is not setup_ph or ph.pool.after[name] > 1:
                    pool.wait_ge(pool_done, value - 1)
                for s, v in waits:
                    pool.wait_ge(s, v)
                issue().then_inc(pool_done, 1)

            def tt(dst, a, b, op):
                return lambda: nc.gpsimd.tensor_tensor(dst, a, b, op)

            def split_queries(ph, head, *waits):
                h = "qa" if head == 0 else "qb"
                lat_rows = slice(LORA, P) if head == 0 else slice(0, LORA)
                pe_rows = slice(0, LORA) if head == 0 else slice(LORA, P)
                for what, src, rows in (("lat", lat, lat_rows), ("pe", pe, pe_rows)):
                    run(ph, f"{h}_{what}_hi", tt(Q_hi[head][rows, :], src[rows, :], ones[rows, :].to_broadcast([LORA, S]), ALU.mult), *waits)
                    run(ph, f"{h}_{what}_lo", tt(Q_lo[head][rows, :], src[rows, :], Q_hi[head][rows, :].bitcast(F32), ALU.subtract))
                    waits = ()

            def weights(ph, pairs):
                free = () if ph is setup_ph else ((slot_ready, ph.base["ready"]),)
                pew = wq_sb[:].rearrange("p k (h c) -> p k h c", h=2)[:, :, :, NOPE:NOPE + ROPE]
                run(ph, "wpe_hi", tt(wpe_hi[:], pew, ones[:].unsqueeze(2).unsqueeze(3).to_broadcast([P, KE, 2, ROPE]), ALU.mult), (wq_loaded, 16 * pairs), *free)
                run(ph, "wpe_lo", tt(wpe_lo[:], pew, wpe_hi[:].bitcast(F32), ALU.subtract))
                run(ph, "wkvs", tt(wkvs[0:LORA, :], wkv_sb[:], scale_sb[:].to_broadcast([LORA, KVW]), ALU.mult),
                    (wkv_loaded, 16 * pairs), (consts_loaded, 64))

            def rotate(ph, step, src, dst, c_buf, s_buf, n, parts, *waits):
                half = ROPE // 2
                tiles = slice(BLK * n, BLK * n + BLK)

                def table(tab, m):
                    return tab[:, tiles, :].unsqueeze(2).to_broadcast([P, BLK, m, half])

                def halves(ap, i):
                    return ap.rearrange("p t (m x d) -> p t m x d", m=parts, x=2)[:, :, :, i, :]

                whole = lambda ap: ap.rearrange("p t (m d) -> p t m d", d=half)
                run(ph, step(0), tt(whole(c_buf), whole(src), table(cos_sb, 2 * parts), ALU.mult), *waits)
                run(ph, step(1), tt(halves(s_buf, 0), halves(src, 1), table(sin_sb, parts), ALU.mult))
                run(ph, step(2), tt(halves(s_buf, 1), halves(src, 0), table(sin_sb, parts), ALU.mult))
                run(ph, step(3), tt(halves(dst, 0), halves(c_buf, 0), halves(s_buf, 0), ALU.subtract))
                run(ph, step(4), tt(halves(dst, 1), halves(c_buf, 1), halves(s_buf, 1), ALU.add))

            def rotate_query(ph, n, pairs):
                c = query_cols(n)
                run(ph, f"rope{n}.0", tt(pe[:, c], q_pe[:], cosT[:, c], ALU.mult), (swapped, NG * (pairs - 1) + n + 1), (tables_loaded, 32))
                run(ph, f"rope{n}.1", tt(q_swap[:], q_swap[:], sinT[:, c], ALU.mult))
                run(ph, f"rope{n}.2", tt(pe[:, c], pe[:, c], q_swap[:], ALU.add))

            def rotate_queries(ph, pairs):
                for n in range(NG):
                    rotate_query(ph, n, pairs)

            def memset(ap, value):
                return lambda: nc.gpsimd.memset(ap, value)

            def key_scale(ph, n):
                c = slice(BLK * n, BLK * n + BLK)
                run(ph, f"rms{n}", tt(rms[:, c], ms_eps[:, c], minus_half[:], ALU.pow), (ms_ready, n + 1))

            def rotate_key(ph, n):
                c = slice(BLK * n, BLK * n + BLK)
                rotate(ph, lambda i: f"kr{n}.{i}", kraw[:, c, LORA:P], krot[:, c, :], krope_c[:, c, :], krope_s[:, c, :], n, 1,
                       (act_freed, ph.after("act", ("kv", n))), (consts_loaded, 64))
                run(ph, f"kr{n}.5", lambda: nc.gpsimd.tensor_scalar(kcat[:, c, LORA:2 * LORA], krot[:, c, :], SCALE, 1.0, ALU.mult, ALU.mult))

            ph = setup_ph
            run(ph, "half", memset(minus_half[:], -0.5))
            run(ph, "ones", memset(ones[:], 1.0))
            run(ph, "ident0", memset(ident[:], 0.0))
            run(ph, "ident", lambda: nc.gpsimd.affine_select(out=ident[:], in_=ident[:], compare_op=ALU.not_equal, fill=1.0,
                                                             base=0, pattern=[[-1, P]], channel_multiplier=1))
            run(ph, "wkvs0", memset(wkvs[LORA:P, :], 0.0))
            run(ph, "wvT0", memset(wvT[:], 0.0))
            run(ph, "v1", memset(v[:, :, LORA:LORA + 1], 1.0))
            run(ph, "identb", lambda: nc.gpsimd.tensor_copy(identb[:], ident[:]))
            run(ph, "mask0", memset(mask[:], 0.0))
            run(ph, "mask", lambda: nc.gpsimd.affine_select(out=mask[:], in_=mask[:], compare_op=ALU.is_ge, fill=MASKED,
                                                            base=0, pattern=[[-1, P]], channel_multiplier=1))
            for n in range(NG):
                c = slice(BLK * n, BLK * n + BLK)
                run(ph, f"rstd{n}", tt(rstd[:, c], var_eps[:, c], minus_half[:], ALU.pow), (var_ready, n + 1))
            weights(ph, 1)
            key_scale(ph, 0)
            rotate_key(ph, 0)
            key_scale(ph, 1)
            rotate_key(ph, 1)
            rotate_query(ph, 0, 1)
            key_scale(ph, 2)
            rotate_key(ph, 2)
            rotate_query(ph, 1, 1)
            key_scale(ph, 3)
            rotate_key(ph, 3)
            rotate_query(ph, 2, 1)
            rotate_query(ph, 3, 1)
            with pool.Fori(0, PAIRS - 1) as p:
                ph = loop_ph.of_pair(p)
                split_queries(ph, 1, (scores_ready, p * STEPS + SBANKS), (act_freed, ph.base["act"]))
                weights(ph, p + 2)
                rotate_queries(ph, p + 2)
                split_queries(ph, 0, (act_freed, ph.after("act", "lat3")),
                              (scores_ready, p * STEPS + NCH))
            split_queries(last_ph, 1, (scores_ready, (PAIRS - 1) * STEPS + SBANKS), (act_freed, last_ph.base["act"]))
            ph = last_ph
            run(ph, "up_zero", lambda: nc.gpsimd.memset(up_raw[:, :, IT - 1, :], 0.0))
            run(ph, "up_scale_zero", lambda: nc.gpsimd.memset(up_scale[:], 0.0))
            run(ph, "down_zero", lambda: nc.gpsimd.memset(down_raw[:, :, INTER:IT * P], 0.0))
            for w in range(2):
                run(ph, f"up_scaled{w}", tt(up_raw[:, w], up_raw[:, w], up_scale[:, w, :].unsqueeze(2).to_broadcast([P, IT, E]), ALU.mult), (ffn_loaded, 16 * 10))
            run(ph, "down_scaled", tt(down_raw[:], down_raw[:], down_scale[:].unsqueeze(2).to_broadcast([P, KE, IT * P]), ALU.mult))

            for j in range(NG * IT):
                n, it = divmod(j, IT)
                pool.wait_ge(hid_hi_done, j + 1)
                nc.gpsimd.tensor_tensor(hid_lo[:, n % 2, it, :], hid[:, j % 2, :], hid_hi[:, n % 2, it, :].bitcast(F32), ALU.subtract).then_inc(hid_lo_done, 1)


_INS = ["L0_attn_x", "L0_attn_wq", "L0_attn_wkv_a", "L0_attn_wkv_b", "L0_attn_wo", "L0_attn_kv_norm_scale",
        "L0_ffn_gate_w", "L0_ffn_up_w", "L0_ffn_down_w", "L0_ffn_gate_s", "L0_ffn_up_s", "L0_ffn_down_s"]


def kernel(**inputs):
    import numpy as _np
    import concourse.bacc as _bacc
    from concourse import mybir as _mybir
    from concourse.bass_utils import run_bass_kernel_spmd as _run

    nc = _bacc.Bacc("TRN2", target_bir_lowering=False, num_devices=1)
    inv = (1.0 / _np.float32(10000.0) ** (_np.arange(0, ROPE, 2, dtype=_np.float32) / _np.float32(ROPE))).astype(_np.float32)
    angle = _np.arange(S, dtype=_np.float32)[:, None] * inv
    arrays = {"cos_dram": _np.cos(angle.astype(_np.float64)).astype(_np.float32),
              "sin_dram": _np.sin(angle.astype(_np.float64)).astype(_np.float32)}
    sign = _np.repeat(_np.float32([-1, 1, -1, 1]), ROPE // 2)[:, None]
    arrays["cosT_dram"] = _np.ascontiguousarray(_np.tile(arrays["cos_dram"].T, (4, 1)))
    arrays["sinT_dram"] = _np.ascontiguousarray(_np.tile(arrays["sin_dram"].T, (4, 1)) * sign)
    args = []
    for name in _INS:
        a = _np.ascontiguousarray(inputs[name])
        arrays[f"in_{name}_dram"] = a
        args.append(nc.dram_tensor(f"in_{name}_dram", a.shape, _mybir.dt.from_np(a.dtype), kind="ExternalInput").ap())
    for name in ("cos_dram", "sin_dram"):
        args.append(nc.dram_tensor(name, (S, ROPE // 2), F32, kind="ExternalInput").ap())
    for name in ("cosT_dram", "sinT_dram"):
        args.append(nc.dram_tensor(name, (P, S), F32, kind="ExternalInput").ap())
    args.append(nc.dram_tensor("out_0_dram", (1, S, E), F32, kind="ExternalOutput").ap())
    mla_gated_ffn_kernel(nc, *args)
    r = _run(nc, [arrays], core_ids=[0])
    return r.results[0]["out_0_dram"]
```
